# Optimizing a Trainium2 kernel written in Bass

```python
import numpy as np
import jax
import jax.numpy as jnp

def _softmax(x, axis=-1):
    return jax.nn.softmax(x, axis=axis)

def _gelu(x):
    return jax.nn.gelu(x, approximate=True)

def _silu(x):
    return jax.nn.silu(x)

def _sigmoid(x):
    return jax.nn.sigmoid(x)

def _layernorm(x, axis=-1, eps=1e-05):
    m = jnp.mean(x, axis=axis, keepdims=True)
    v = jnp.var(x, axis=axis, keepdims=True)
    return (x - m) / jnp.sqrt(v + eps)

def _scatter_add(tgt, idx, src, axis=0):
    return tgt.at[idx].add(src)

def _segment_sum(src, seg, n):
    return jax.ops.segment_sum(src, seg, n)
kernel_name = 'mk_prb_d1_jaxref_r8_b8db9f'

def setup_inputs(seed: int=0):
    np.random.seed(seed)
    _w = jnp.asarray

    def _L0_attn_setup():
        import jax, jax.numpy as jnp
        import numpy as np
        WIDTH = 256
        NUM_HEADS = 16
        HEAD_DIM = WIDTH // NUM_HEADS
        ROPE_DIMS = HEAD_DIM // 2
        WINDOW = 64
        ROPE_BASE = 10000.0
        NEG_INF = -1000000000.0

        def apply_rope(x, dims, offset=0, base=ROPE_BASE):
            L = x.shape[2]
            half = dims // 2
            pos = (offset + jnp.arange(L)).astype(x.dtype)
            inv_freq = jnp.exp(-jnp.log(jnp.asarray(base, x.dtype)) * (jnp.arange(0, dims, 2).astype(x.dtype) / dims))
            theta = pos[:, None] * inv_freq[None, :]
            cos = jnp.cos(theta)[None, None]
            sin = jnp.sin(theta)[None, None]
            x1 = x[..., :half]
            x2 = x[..., half:dims]
            rest = x[..., dims:]
            rx1 = x1 * cos - x2 * sin
            rx2 = x1 * sin + x2 * cos
            return jnp.concatenate([rx1, rx2, rest], axis=-1)
        key = jax.random.key(seed)
        ks = jax.random.split(key, 6)
        B, L, D, hd = (2, 256, WIDTH, HEAD_DIM)
        x = jax.random.normal(ks[0], (B, L, D), dtype=jnp.float32)
        Wq = jax.random.normal(ks[1], (D, D), dtype=jnp.float32) * 0.02
        Wk = jax.random.normal(ks[2], (D, hd), dtype=jnp.float32) * 0.02
        Wv = jax.random.normal(ks[3], (D, hd), dtype=jnp.float32) * 0.02
        Wo = jax.random.normal(ks[4], (D, D), dtype=jnp.float32) * 0.02
        bo = jax.random.normal(ks[5], (D,), dtype=jnp.float32) * 0.02
        return {'x': x, 'Wq': Wq, 'Wk': Wk, 'Wv': Wv, 'Wo': Wo, 'bo': bo}
    _L0_attn_in = _L0_attn_setup()

    def _L0_ffn_setup():
        import jax, jax.numpy as jnp
        import numpy as np
        B, T, D = (2, 128, 256)
        E, F, K = (64, 64, 4)
        S, HS = (2, 64 * 4)
        key = jax.random.key(seed)
        ks = jax.random.split(key, 9)
        s = 0.02
        f32 = jnp.float32
        return {'x': jax.random.normal(ks[0], (B, T, D), f32), 'router_w': jax.random.normal(ks[1], (D, E), f32) * s, 'router_bias': jnp.zeros((E,), f32), 'wg': jax.random.normal(ks[2], (E, D, F), f32) * s, 'wu': jax.random.normal(ks[3], (E, D, F), f32) * s, 'wd': jax.random.normal(ks[4], (E, F, D), f32) * s, 'swg': jax.random.normal(ks[5], (S, D, HS), f32) * s, 'swu': jax.random.normal(ks[6], (S, D, HS), f32) * s, 'swd': jax.random.normal(ks[7], (S, HS, D), f32) * s}
    _L0_ffn_in = _L0_ffn_setup()
    _d = {'L0_attn_x': _L0_attn_in['x'], 'L0_attn_Wq': _L0_attn_in['Wq'], 'L0_attn_Wk': _L0_attn_in['Wk'], 'L0_attn_Wv': _L0_attn_in['Wv'], 'L0_attn_Wo': _L0_attn_in['Wo'], 'L0_attn_bo': _L0_attn_in['bo'], 'L0_ffn_router_w': _L0_ffn_in['router_w'], 'L0_ffn_router_bias': _L0_ffn_in['router_bias'], 'L0_ffn_wg': _L0_ffn_in['wg'], 'L0_ffn_wu': _L0_ffn_in['wu'], 'L0_ffn_wd': _L0_ffn_in['wd'], 'L0_ffn_swg': _L0_ffn_in['swg'], 'L0_ffn_swu': _L0_ffn_in['swu'], 'L0_ffn_swd': _L0_ffn_in['swd']}
    _x0 = _d['L0_attn_x']
    _d['L0_attn_x'] = jax.random.normal(jax.random.fold_in(jax.random.key(seed), 1), (4, 512, 256), dtype=_x0.dtype)
    del _x0
    return _d

def reference(L0_attn_x, L0_attn_Wq, L0_attn_Wk, L0_attn_Wv, L0_attn_Wo, L0_attn_bo, L0_ffn_router_w, L0_ffn_router_bias, L0_ffn_wg, L0_ffn_wu, L0_ffn_wd, L0_ffn_swg, L0_ffn_swu, L0_ffn_swd):

    def _L0_attn_ref(x, Wq, Wk, Wv, Wo, bo):
        import jax, jax.numpy as jnp
        import numpy as np
        WIDTH = 256
        NUM_HEADS = 16
        HEAD_DIM = WIDTH // NUM_HEADS
        ROPE_DIMS = HEAD_DIM // 2
        WINDOW = 64
        ROPE_BASE = 10000.0
        NEG_INF = -1000000000.0

        def apply_rope(x, dims, offset=0, base=ROPE_BASE):
            L = x.shape[2]
            half = dims // 2
            pos = (offset + jnp.arange(L)).astype(x.dtype)
            inv_freq = jnp.exp(-jnp.log(jnp.asarray(base, x.dtype)) * (jnp.arange(0, dims, 2).astype(x.dtype) / dims))
            theta = pos[:, None] * inv_freq[None, :]
            cos = jnp.cos(theta)[None, None]
            sin = jnp.sin(theta)[None, None]
            x1 = x[..., :half]
            x2 = x[..., half:dims]
            rest = x[..., dims:]
            rx1 = x1 * cos - x2 * sin
            rx2 = x1 * sin + x2 * cos
            return jnp.concatenate([rx1, rx2, rest], axis=-1)
        B, L, D = x.shape
        H, hd = (NUM_HEADS, HEAD_DIM)
        scale = hd ** (-0.5)
        q = (x @ Wq).reshape(B, L, H, hd).transpose(0, 2, 1, 3)
        k = (x @ Wk).reshape(B, L, 1, hd).transpose(0, 2, 1, 3)
        v = (x @ Wv).reshape(B, L, 1, hd).transpose(0, 2, 1, 3)
        q = apply_rope(q, ROPE_DIMS)
        k = apply_rope(k, ROPE_DIMS)
        i = jnp.arange(L)[:, None]
        j = jnp.arange(L)[None, :]
        allowed = (i - j >= 0) & (i - j < WINDOW)
        mask = jnp.where(allowed, 0.0, NEG_INF).astype(x.dtype)
        scores = jnp.einsum('bhqd,bkd->bhqk', q, k[:, 0]) * scale
        scores = scores + mask[None, None]
        attn = jax.nn.softmax(scores, axis=-1)
        out = jnp.einsum('bhqk,bkd->bhqd', attn, v[:, 0])
        out = out.transpose(0, 2, 1, 3).reshape(B, L, D)
        return out @ Wo + bo

    def _L0_ffn_ref(x, router_w, router_bias, wg, wu, wd, swg, swu, swd):
        import jax, jax.numpy as jnp
        import numpy as np
        B, T, D = (2, 128, 256)
        E, F, K = (64, 64, 4)
        S, HS = (2, 64 * 4)
        b, t, d = x.shape
        flat = x.reshape(b * t, d)
        n = flat.shape[0]
        logits = flat @ router_w
        scores = jax.nn.softmax(logits, axis=-1)
        _, topk_idx = jax.lax.top_k(logits + router_bias, K)
        topk_scores = jnp.take_along_axis(scores, topk_idx, axis=-1)
        topk_scores = topk_scores / topk_scores.sum(axis=-1, keepdims=True)
        comb = jnp.zeros((n, E), dtype=flat.dtype).at[jnp.arange(n)[:, None], topk_idx].set(topk_scores)
        g = jax.nn.silu(jnp.einsum('nd,edf->nef', flat, wg))
        u = jnp.einsum('nd,edf->nef', flat, wu)
        routed = jnp.einsum('ne,nef,efd->nd', comb, g * u, wd)
        sg = jax.nn.silu(jnp.einsum('nd,sdh->nsh', flat, swg))
        su = jnp.einsum('nd,sdh->nsh', flat, swu)
        shared = jnp.einsum('nsh,shd->nd', sg * su, swd)
        return (routed + shared).reshape(b, t, d)
    x = L0_attn_x
    xn = _layernorm(x, axis=-1)
    x = x + _L0_attn_ref(xn, L0_attn_Wq, L0_attn_Wk, L0_attn_Wv, L0_attn_Wo, L0_attn_bo) + _L0_ffn_ref(xn, L0_ffn_router_w, L0_ffn_router_bias, L0_ffn_wg, L0_ffn_wu, L0_ffn_wd, L0_ffn_swg, L0_ffn_swu, L0_ffn_swd)
    return x

_drawn_inputs = setup_inputs


def setup_inputs(seed=0):
    import zlib

    import numpy as np

    out = dict(_drawn_inputs(seed))
    spreads = {'L0_ffn_router_bias': (0.0, 0.8)}
    factors = {'L0_attn_Wq': 8.0,
     'L0_attn_Wk': 8.0,
     'L0_attn_Wv': 3.671,
     'L0_attn_Wo': 3.648,
     'L0_attn_bo': 45.002,
     'L0_ffn_router_w': 8.0,
     'L0_ffn_wg': 8.0,
     'L0_ffn_wu': 8.0,
     'L0_ffn_wd': 8.0,
     'L0_ffn_swg': 8.0,
     'L0_ffn_swu': 8.0,
     'L0_ffn_swd': 8.0}
    for name, (base, spread) in spreads.items():
        noise = np.random.default_rng([zlib.crc32(name.encode()), seed]).standard_normal(out[name].shape)
        drawn = base * np.exp(spread * noise) if base else spread * noise
        out[name] = jnp.asarray(drawn.astype(out[name].dtype))
    for name, factor in factors.items():
        out[name] = (out[name] * factor).astype(out[name].dtype)
    return out
```

```python
from contextlib import ExitStack

import numpy as np

import concourse.bass as bass
from concourse import mybir

B, L, D = 4, 512, 256
H, HD = 16, 16
ROT = HD // 4
WINDOW = 64
ROPE_BASE = 10000.0
MASKED = -1.0e9
E, F, TOPK = 64, 64, 4
S, HS = 2, 256
P = 128
NT = B * L // P
TPB = L // P
NC = D // P
QB = P // WINDOW
NBLK = (NT * P * TOPK - E) // P + E
NQK = (H + 1) * HD
NPROJ = NQK + HD + E
FC = S * HS // P
QPARTS = (0, 0, 0, 1, 1, 2)
KPARTS = (0, 1, 2, 0, 1, 0)
SROWS = len(QPARTS) * HD
MROWS = 2
GT = 2
EPS = 1e-5


def layout_constants():
    pos = np.arange(L, dtype=np.float32)
    inv = np.exp(-np.log(np.float32(ROPE_BASE)) * (np.arange(0, 2 * ROT, 2).astype(np.float32) / np.float32(2 * ROT))).astype(np.float32)
    theta = (pos[:, None] * inv[None, :]).astype(np.float32)
    part = np.arange(P)
    rows = lambda a: np.ascontiguousarray(a.reshape(TPB, P, ROT).transpose(1, 0, 2).reshape(P, TPB * ROT))
    f32 = {
        "ident": np.eye(P),
        "cos": rows(np.cos(theta)),
        "sin": rows(np.sin(theta)),
        "experts": np.tile(np.arange(E), (P, 1)),
        "token": part[:, None] + P * np.arange(NT)[None, :],
        "row": part[:, None],
        "half": (part // F)[:, None],
    }
    q, j = part % WINDOW, np.arange(P)
    band = (j[None, :] > q[:, None]) & (j[None, :] <= q[:, None] + WINDOW)
    first = band & (j[None, :] >= WINDOW)
    top = (part < WINDOW)[:, None]
    cost = lambda ok: np.where(ok, 0.0, MASKED)
    b16 = {
        "identb": np.eye(P),
        "mask": cost(band),
        "mask_first": cost(first),
        "maskT": np.where(top, cost(band), 0.0),
        "maskT_first": np.where(top, cost(first), 0.0),
        "spread": np.tile(np.where(top, np.eye(P)[:, :WINDOW], 0.0), (1, H // 2)),
        "before": (part[:, None] < part[None, :]),
        "ones": np.ones((P, P)),
        "ramp": np.tile(np.arange(P), (P, 1)),
    }
    pack = lambda d: ({n: a.shape[1] for n, a in d.items()}, np.concatenate([np.asarray(a, np.float32) for a in d.values()], 1))
    w32, a32 = pack(f32)
    w16, a16 = pack(b16)
    return (w32, a32), (w16, (a16.view(np.uint32) >> 16).astype(np.uint16))


def build(nc, x, Wq, Wk, Wv, Wo, bo, router_w, router_bias, wg, wu, wd, swg, swu, swd, c32, c16, w32, w16, out):
    f32, f32r, bf16, f16 = mybir.dt.float32, mybir.dt.float32r, mybir.dt.bfloat16, mybir.dt.float16
    i32, u32 = mybir.dt.int32, mybir.dt.uint32
    ALU, ACT, AX = mybir.AluOpType, mybir.ActivationFunctionType, mybir.AxisListType
    pe, dve, act, pool, sp = nc.tensor, nc.vector, nc.scalar, nc.gpsimd, nc.sync
    ctx = ExitStack()

    sems, count, at, seen = {}, {}, {}, {}

    def did(ins, step, item=None, by=1):
        if step not in sems:
            sems[step], count[step] = ctx.enter_context(nc.semaphore("s_" + step)), 0
        ins.then_inc(sems[step], by)
        count[step] += by
        at[step, item] = count[step]
        return ins

    def need(eng, step, item=None):
        v = at[step, item]
        if seen.get((eng.engine, step), 0) < v:
            seen[eng.engine, step] = v
            eng.wait_ge(sems[step], v)

    def landed(ins, step, item=None):
        return did(ins, step, item, 16)

    def sb(name, shape, dt=f32):
        return ctx.enter_context(nc.sbuf_tensor(name, shape, dt))

    bank = [ctx.enter_context(nc.psum_tensor(f"bank{i}", [P, 512], f32)) for i in range(8)]
    cf, cb = sb("cf", [P, c32.shape[1]]), sb("cb", [P, c16.shape[1]], bf16)
    wproj = sb("wproj", [P, NC, NPROJ])
    wsh = sb("wsh", [P, NC, 2, S, HS])
    wshd = sb("wshd", [P, FC, D])
    wo_sb = sb("wo_sb", [P, NC, D])
    wgu = sb("wgu", [P, E * 2 * NC * F])
    wdn = sb("wdn", [P, E // 2 * D])
    xnT = sb("xnT", [P, NC, NT * P])
    aT = sb("aT", [P, NC * NT * P])
    qS = sb("qS", [P, 2, QB, H, WINDOW], bf16)
    kS = sb("kS", [P, 2, WINDOW + L], bf16)
    bias_sb = sb("bias_sb", [P, E])
    pos_f, pos_i = sb("pos_f", [P, NT, TOPK]), sb("pos_i", [P, NT, TOPK], i32)
    gate = sb("gate", [P, NT, TOPK])
    slot_token = sb("slot_token", [P, P], i32)
    wslice = sb("wslice", [1, 2, P], i32)
    halfmask = sb("halfmask", [P, P])
    small = sb("small", [P, 1152])
    arena = sb("arena", [P, 10500])
    xn_d = nc.dram_tensor("xn_d", (NT * P, D), f32, kind="Internal").ap()
    y_d = nc.dram_tensor("y_d", (NBLK * P, D), f32, kind="Internal").ap()

    def columns(t, widths):
        r, o = {}, 0
        for n, w in widths.items():
            r[n] = t[:, o:o + w]
            o += w
        return r

    k32, k16 = columns(cf, w32), columns(cb, w16)
    ident = k32["ident"]

    class Region:

        def __init__(self, t):
            self.t, self.o = t, 0

        def take(self, n, dt=f32):
            words = n if dt in (f32, f32r, i32, u32) else n // 2
            v = self.t[:, self.o:self.o + words]
            self.o += words
            assert self.o <= self.t.shape[1], (self.o, self.t.shape)
            return v if dt == f32 else v.bitcast(dt)

    sm = Region(small)
    stats = sm.take(TPB * 6).rearrange("p (t s) -> p t s", s=6)
    mv = sm.take(NT * 2).rearrange("p (t s) -> p t s", s=2)
    var, rstd, newt = sm.take(NT), sm.take(NT), sm.take(NT)
    top8 = sm.take(NT * 8).rearrange("p (t k) -> p t k", k=8)
    arg8 = sm.take(NT * 8, u32).rearrange("p (t k) -> p t k", k=8)
    pick = sm.take(TOPK * NT).rearrange("p (k t) -> p k t", k=TOPK)
    nblk, ends, starts, cmp = sm.take(E), sm.take(E), sm.take(E), sm.take(E)
    blk_expert, tmp1 = sm.take(1), sm.take(4)
    slot_blk, slot_row = sm.take(NT * TOPK), sm.take(NT * TOPK)
    esum, emax = sm.take(NT), sm.take(NT)
    brow = sm.take(2 * P)

    x_b = x.rearrange("b (t p) d -> b p t d", p=P)
    xio = Region(wgu)
    x_in = [xio.take(TPB * D).rearrange("p (t d) -> p t d", d=D) for _ in range(B)]
    x_n = [xio.take(TPB * D).rearrange("p (t d) -> p t d", d=D) for _ in range(B)]
    for b in range(B):
        landed(sp.dma_start(x_in[b], x_b[b]), f"x{b}")
    rows = lambda w: w.rearrange("(p c) n -> p c n", c=NC)
    landed(act.dma_start(cf[:, :], c32), "c32")
    col = 0
    for i, (w, n) in enumerate(((Wq, H * HD), (Wk, HD), (Wv, HD), (router_w, E))):
        landed(act.dma_start(wproj[:, :, col:col + n], rows(w)), "wproj", i)
        col += n
    landed(act.dma_start(cb[:, :].bitcast(mybir.dt.uint16), c16), "c16")
    landed(act.dma_start(bias_sb[:, :], router_bias.partition_broadcast(P)), "bias")

    ar = Region(arena)
    qk = ar.take(NT * NQK).rearrange("p (t h d) -> p t h d", h=H + 1, d=HD)
    qtok = [ar.take(H * SROWS, bf16).rearrange("p (h c d) -> p h c d", h=H, d=HD) for _ in range(2)]
    used_words = ar.o
    rt = Region(wdn)
    logit = rt.take(NT * E).rearrange("p (t e) -> p t e", e=E)
    biased = rt.take(NT * E).rearrange("p (t e) -> p t e", e=E)
    v0 = ar.take(NT * 32).rearrange("p (t d) -> p t d", d=32)
    v1 = ar.take(NT * 32).rearrange("p (t d) -> p t d", d=32)
    did(pool.memset(v0[:, :, :], 1.0), "v_fill")
    did(pool.memset(v1[:, :, :], 1.0), "v_fill")
    need(pool, "v_fill")
    did(pool.memset(v1[0:WINDOW, :, 0:HD], 0.0), "v_fill")

    def normalize(b):
        need(dve, f"x{b}")
        ts = slice(b * TPB, (b + 1) * TPB)
        for t in range(TPB):
            if b:
                need(dve, "moments", b * TPB + t - TPB)
            did(dve.bn_stats(stats[:, t, :], x_in[b][:, t, :]), "stats", b * TPB + t)
        for t in range(TPB):
            need(dve, "stats", b * TPB + t)
            did(dve.bn_aggr(mv[:, b * TPB + t, :], stats[:, t, :]), "moments", b * TPB + t)
        need(dve, "moments", b * TPB + TPB - 1)
        did(dve.tensor_scalar(var[:, ts], mv[:, ts, 1], EPS, None, ALU.add), "var", b)
        need(act, "var", b)
        did(act.activation(newt[:, ts], var[:, ts], ACT.Sqrt), "root", b)
        need(dve, "root", b)
        did(dve.reciprocal(rstd[:, ts], newt[:, ts]), "rs", (b, 0))
        need(dve, "rs", (b, 0))
        did(dve.tensor_tensor(newt[:, ts], rstd[:, ts], rstd[:, ts], ALU.mult), "rs", (b, 1))
        need(dve, "rs", (b, 1))
        did(dve.tensor_tensor(newt[:, ts], newt[:, ts], var[:, ts], ALU.mult), "rs", (b, 2))
        need(dve, "rs", (b, 2))
        did(dve.tensor_scalar(newt[:, ts], newt[:, ts], -0.5, 1.5, ALU.mult, ALU.add), "rs", (b, 3))
        need(dve, "rs", (b, 3))
        did(dve.tensor_tensor(rstd[:, ts], rstd[:, ts], newt[:, ts], ALU.mult), "rs", (b, 4))
        need(dve, "rs", (b, 4))
        for t in range(TPB):
            T = b * TPB + t
            did(dve.tensor_scalar(x_n[b][:, t, :], x_in[b][:, t, :], mv[:, T, 0:1], rstd[:, T:T + 1],
                                  ALU.subtract, ALU.mult), "normed", T)
        need(sp, "normed", b * TPB + TPB - 1)
        landed(sp.dma_start(xn_d[b * L:(b + 1) * L, :].rearrange("(t p) d -> p t d", p=P), x_n[b]), f"xn{b}")

    def transpose_x(T):
        b, t = divmod(T, TPB)
        need(pe, "c32")
        need(pe, "normed", T)
        if T >= 2:
            need(pe, "xT_out", T - 2)
        for c in range(NC):
            ins = pe.transpose(bank[T % 2][:, c * P:(c + 1) * P], x_n[b][:, t, c::NC], ident)
        did(ins, "x_T", T)
        need(act, "x_T", T)
        did(act.activation(xnT[:, :, T * P:(T + 1) * P], bank[T % 2][:, 0:D].rearrange("p (c n) -> p c n", c=NC),
                           ACT.Copy), "xT_out", T)

    def project(T):
        need(pe, "wproj", 3)
        need(pe, "xT_out", T)
        if T >= 2:
            need(pe, "proj_qk", T - 2)
            need(pe, "proj_v", T - 2)
        o = bank[2 + T % 2]
        for c in range(NC):
            ins = pe.matmul(o[:, 0:NPROJ], xnT[:, c, T * P:(T + 1) * P], wproj[:, c, :],
                            start=c == 0, stop=c == NC - 1)
        did(ins, "proj", T)
        need(act, "proj", T)
        did(act.activation(qk[:, T].rearrange("p h d -> p (h d)"), o[:, 0:NQK], ACT.Copy), "proj_qk", T)
        need(dve, "proj_qk", T)
        if T == 0:
            need(dve, "v_fill")
        did(dve.tensor_copy(logit[:, T, :], o[:, NQK + HD:NPROJ]), "logit", T)
        did(dve.tensor_copy(v0[:, T, 0:HD], o[:, NQK:NQK + HD]), "proj_v", T)

    def load_shared():
        for g, w in enumerate((swg, swu)):
            for n in range(S):
                landed(sp.dma_start(wsh[:, :, g, n, :], rows(w[n])), "wsh", (g, n))
        landed(sp.dma_start(wshd[:, :, :], swd.rearrange("s (k p) d -> p (s k) d", p=P)), "wshd")
        for g in range(4):
            for j in range(4):
                r = (4 * g + j) * HD
                h = 4 * j + g
                landed(sp.dma_start(wo_sb[r % P:r % P + HD, r // P, :], Wo[h * HD:(h + 1) * HD, :]), "wo", r)

    wgu_v = wgu[:, :].rearrange("p (e g c f) -> p e g c f", e=E, g=2, c=NC)
    EG = 8

    def load_gate_up(groups):
        for b in range(B):
            need(sp, f"xn{b}")
        need(sp, "x_T", NT - 1)
        need(sp, "normed", NT - 1)
        for i in groups:
            for g, w in enumerate((wg, wu)):
                src = w[i * EG:(i + 1) * EG].rearrange("e (p c) f -> p e c f", c=NC)
                landed(sp.dma_start(wgu_v[:, i * EG:(i + 1) * EG, g], src), "wgu", (i, g))
                yield

    def load_down():
        wdn_v = wdn[:, :].rearrange("p (j d) -> p j d", d=D)
        need(sp, "gate")
        for j in range(0, E // 2, EG):
            for h in range(2):
                e = h * E // 2 + j
                landed(sp.dma_start(wdn_v[h * F:(h + 1) * F, j:j + EG], wd[e:e + EG].rearrange("j f d -> f j d")),
                       "wdn", (j, h))
                yield

    onehot = rt.take(TOPK * NT * E, bf16).rearrange("p (k t e) -> p k t e", k=TOPK, e=E)
    member = rt.take(NT * E, bf16).rearrange("p (t e) -> p t e", e=E)
    earlier = rt.take((NT + 1) * E, bf16).rearrange("p (t e) -> p t e", e=E)
    product = rt.take(NT * E).rearrange("p (t e) -> p t e", e=E)
    expo = biased
    table = brow[:, 0:P]
    NR = 12
    who = [rt.take(P, f16) for _ in range(NR)]
    where = [rt.take(P, f16) for _ in range(NR)]
    small_bank = bank[6]
    small16 = small_bank[:, :].bitcast(bf16)
    small_reader = [None]

    def small_free():
        if small_reader[0]:
            need(pe, *small_reader[0])

    MAGIC = float(1.5 * 2 ** 23)
    route_n = [0]

    def chain(ins):
        route_n[0] += 1
        did(ins, "route", route_n[0])
        need(dve, "route", route_n[0])

    def named(step):
        at[step, None], sems[step] = at["route", route_n[0]], sems["route"]

    over_tiles = lambda v: v.unsqueeze(1).to_broadcast([P, NT, E])
    over_k = lambda v: v.unsqueeze(2).to_broadcast([P, NT, TOPK])

    def routing():
        need(dve, "bias")
        need(dve, "c32")
        need(dve, "c16")
        need(dve, "logit", NT - 1)
        chain(dve.tensor_tensor(biased, logit, over_tiles(bias_sb[:, :]), ALU.add))
        yield
        for t in range(NT):
            ins = dve.max(top8[:, t, :], biased[:, t, :])
            if t % 8 == 7:
                chain(ins)
                yield
        for t in range(NT):
            ins = dve.max_index(arg8[:, t, :], top8[:, t, :], biased[:, t, :])
            if t % 8 == 7:
                chain(ins)
                yield
        chain(dve.tensor_copy(pick, arg8[:, :, 0:TOPK].rearrange("p t k -> p k t")))
        for k in range(TOPK):
            chain(dve.tensor_tensor(onehot[:, k], over_tiles(k32["experts"]),
                                    pick[:, k, :].unsqueeze(2).to_broadcast([P, NT, E]), ALU.is_equal))
            yield
        chain(dve.tensor_tensor(member, onehot[:, 0], onehot[:, 1], ALU.add))
        chain(dve.tensor_tensor(member, member, onehot[:, 2], ALU.add))
        yield
        chain(dve.tensor_tensor(member, member, onehot[:, 3], ALU.add))
        chain(dve.memset(earlier[:, 0, :], 0.0))
        yield
        for t in range(NT):
            chain(dve.tensor_tensor(earlier[:, t + 1, :], earlier[:, t, :], member[:, t, :], ALU.add))
            if t % 4 == 3:
                yield
        named("earlier")
        yield
        need(pe, "c16")
        need(pe, "earlier")
        small_free()
        total = small_bank[:, 0:E]
        did(pe.matmul(total, k16["ones"], earlier[:, NT, :], start=True, stop=True), "totals")
        need(dve, "totals")
        chain(dve.tensor_scalar(nblk, total, 1.0 / P, 0.5 - 1.0 / (2 * P), ALU.mult, ALU.add))
        named("totals_read")
        small_reader[0] = ("totals_read", None)
        chain(dve.tensor_scalar(nblk, nblk, MAGIC, None, ALU.add))
        chain(dve.tensor_scalar(nblk, nblk, MAGIC, None, ALU.subtract))
        chain(dve.memset(cmp, 1.0))
        chain(dve.tensor_tensor_scan(ends, cmp, nblk, 0.0, ALU.mult, ALU.add))
        chain(dve.tensor_tensor(starts, ends, nblk, ALU.subtract))
        chain(dve.tensor_scalar(starts, starts, float(P), None, ALU.mult))
        yield
        for i in range(2):
            small_free()
            ranks = small_bank[:, :].rearrange("p (t e) -> p t e", e=E)
            for t in range(8 * i, 8 * i + 8):
                pe.matmul(ranks[:, t % 8, :], k16["before"], member[:, t, :], start=True, stop=False)
                ins = pe.matmul(ranks[:, t % 8, :], k16["ones"], earlier[:, t, :], start=False, stop=True)
            did(ins, "ranked", i)
            need(dve, "ranked", i)
            chain(dve.tensor_tensor(biased[:, 8 * i:8 * i + 8, :], ranks,
                                    starts.unsqueeze(1).to_broadcast([P, 8, E]), ALU.add))
            at["rank_read", i], sems["rank_read"] = at["route", route_n[0]], sems["route"]
            small_reader[0] = ("rank_read", i)
            yield
        for k in range(TOPK):
            chain(dve.tensor_tensor(product, onehot[:, k], biased, ALU.mult))
            yield
            chain(dve.tensor_reduce(pos_f[:, :, k], product, AX.X, ALU.add))
            yield
        flat_pos = pos_f[:, :, :].rearrange("p t k -> p (t k)")
        chain(dve.tensor_scalar(slot_blk, flat_pos, 1.0 / P, -(0.5 - 1.0 / (2 * P)), ALU.mult, ALU.add))
        chain(dve.tensor_scalar(slot_blk, slot_blk, MAGIC, None, ALU.add))
        chain(dve.tensor_scalar(slot_blk, slot_blk, MAGIC, None, ALU.subtract))
        chain(dve.scalar_tensor_tensor(slot_row, slot_blk, -float(P), flat_pos, ALU.mult, ALU.add))
        need(pool, "route", route_n[0])
        GR = 4
        for i0 in range(0, NT * TOPK + 2 * GR, GR):
            for i in range(i0, i0 + GR if i0 < NT * TOPK else i0):
                if i >= NR:
                    need(dve, "tabled", i0 - NR)
                    need(pool, "tabled", i0 - NR)
                eng, step = ((pool, "where"), (dve, "who"))[i % 2]
                did(eng.tensor_scalar(where[i % NR], k16["ramp"], slot_row[:, i:i + 1], None, ALU.is_equal), step, ("where", i))
                did(dve.tensor_scalar(who[i % NR], k16["ramp"], slot_blk[:, i:i + 1],
                                      k32["token"][:, i // TOPK:i // TOPK + 1], ALU.is_equal, ALU.mult), "who", i)
                if i % 2:
                    yield
            j0 = i0 - 2 * GR
            if j0 < 0:
                continue
            small_free()
            for j in range(j0, j0 + GR):
                if j % 2 == 0:
                    need(pe, "where", ("where", j))
                need(pe, "who", j)
                ins = pe.matmul(small_bank[:, 0:P], where[j % NR], who[j % NR], start=j == j0, stop=j == j0 + GR - 1)
            did(ins, "tabled", j0)
            need(dve, "tabled", j0)
            if j0 == 0:
                chain(dve.tensor_copy(table, small_bank[:, 0:P]))
            else:
                chain(dve.tensor_tensor(table, table, small_bank[:, 0:P], ALU.add))
            named(f"table_read{j0}")
            small_reader[0] = (f"table_read{j0}", None)
        chain(dve.tensor_copy(slot_token[:, :], table))
        did(dve.tensor_copy(pos_i[:, :, :], pos_f[:, :, :]), "slots")
        yield
        chain(dve.tensor_scalar(cmp, ends, k32["row"], None, ALU.is_le))
        chain(dve.tensor_reduce(blk_expert, cmp, AX.X, ALU.add))
        chain(dve.tensor_scalar(blk_expert, blk_expert, float(E - 1), None, ALU.min))
        diag, onesf = brow[:, 0:P], brow[:, P:2 * P]
        chain(dve.tensor_scalar(diag, ident, blk_expert, None, ALU.mult))
        chain(dve.memset(onesf, 1.0))
        named("diag")
        yield
        small_free()
        need(pe, "diag")
        expert_row = small_bank[:, 0:P]
        did(pe.matmul(expert_row, onesf, diag, start=True, stop=True), "expert_row")
        need(dve, "expert_row")
        chain(dve.tensor_scalar(diag, expert_row, float(E // 2), None, ALU.is_ge))
        chain(dve.tensor_scalar(halfmask[:, :], diag, k32["half"], None, ALU.is_equal))
        chain(dve.scalar_tensor_tensor(onesf, diag, -float(E // 2), expert_row, ALU.mult, ALU.add))
        chain(dve.tensor_scalar(wslice[0:1, 0, :], expert_row[0:1, :], 2.0 * NC * F, None, ALU.mult))
        chain(dve.tensor_scalar(wslice[0:1, 1, :], onesf[0:1, :], float(D), None, ALU.mult))
        named("wslice")
        small_reader[0] = ("wslice", None)
        yield
        chain(dve.tensor_reduce(emax, logit, AX.X, ALU.max))
        chain(dve.tensor_tensor(expo, logit, emax.unsqueeze(2).to_broadcast([P, NT, E]), ALU.subtract))
        named("shifted")
        yield
        need(act, "shifted")
        did(act.activation(expo, expo, ACT.Exp), "expo")
        yield
        need(dve, "expo")
        chain(dve.tensor_reduce(esum, expo, AX.X, ALU.add))
        chain(dve.reciprocal(esum, esum))
        yield
        for k in range(TOPK):
            chain(dve.tensor_tensor(product, onehot[:, k], expo, ALU.mult))
            yield
            chain(dve.tensor_reduce(gate[:, :, k], product, AX.X, ALU.add))
            yield
        chain(dve.tensor_tensor(gate[:, :, :], gate[:, :, :], over_k(esum), ALU.mult))
        chain(dve.tensor_reduce(emax, gate[:, :, :], AX.X, ALU.add))
        chain(dve.reciprocal(emax, emax))
        did(dve.tensor_tensor(gate[:, :, :], gate[:, :, :], over_k(emax), ALU.mult), "gate")

    ktok = [ar.take(SROWS + MROWS, bf16) for _ in range(2)]
    probs = [ar.take(H * WINDOW) for _ in range(2)]
    oT = ar.take(4 * P).rearrange("p (g n) -> p g n", g=4)
    rope = [ar.take((H + 1) * ROT).rearrange("p (h d) -> p h d", d=ROT) for _ in range(4)]
    rest = [ar.take((H + 1) * HD).rearrange("p (h d) -> p h d", d=HD) for _ in range(2)]
    spent = Region(wproj[:, :, :].rearrange("p c n -> p (c n)"))
    a_tok = spent.take(D)
    maxf = [spent.take(H) for _ in range(2)]
    maxrest = spent.take(H)
    negmax = [spent.take(MROWS * H, bf16).rearrange("p (m n) -> p m n", m=MROWS) for _ in range(2)]
    negmaxT = [spent.take(P, bf16) for _ in range(2)]
    rden = spent.take(H)
    for i in range(2):
        did(pool.memset(ktok[i][:, :], 1.0), "fill", ("k", i))
        did(pool.memset(kS[:, i, 0:WINDOW], 0.0), "fill", ("kS", i))
    need(pool, "fill", ("kS", 1))
    identb = k16["identb"]
    pool_n = [0]

    def pchain(ins):
        pool_n[0] += 1
        did(ins, "prep", pool_n[0])
        need(pool, "prep", pool_n[0])

    def rotate(T):
        t = T % TPB
        need(pool, "c32")
        need(pool, "proj_qk", T)
        x1, x2 = qk[:, T, :, 0:ROT], qk[:, T, :, ROT:2 * ROT]
        cs = k32["cos"][:, t * ROT:(t + 1) * ROT].unsqueeze(1).to_broadcast([P, H + 1, ROT])
        sn = k32["sin"][:, t * ROT:(t + 1) * ROT].unsqueeze(1).to_broadcast([P, H + 1, ROT])
        if T:
            need(pool, "k_split", T - 1)
        pool.tensor_tensor(rope[0], x1, cs, ALU.mult)
        pool.tensor_tensor(rope[1], x2, sn, ALU.mult)
        pool.tensor_tensor(rope[2], x1, sn, ALU.mult)
        pchain(pool.tensor_tensor(rope[3], x2, cs, ALU.mult))
        pool.tensor_tensor(x1, rope[0], rope[1], ALU.subtract)
        pchain(pool.tensor_tensor(x2, rope[2], rope[3], ALU.add))
        at["roped", T], sems["roped"] = at["prep", pool_n[0]], sems["prep"]
        yield
        q, k = qk[:, T, 0:H, :], qk[:, T, H, :]
        qt, kt = qtok[T % 2], ktok[T % 2]
        if T >= 2:
            need(pool, "k_T", T - 2)
            need(act, "q_T", (T - 2, 1))
        pchain(pool.tensor_scalar(k, k, HD ** -0.5, None, ALU.mult))
        k_parts = lambda part: [kt[:, i * HD:(i + 1) * HD] for i, x in enumerate(KPARTS) if x == part]
        src_q, src_k = q, k
        for part in range(3):
            n = QPARTS.count(part)
            first = QPARTS.index(part)
            need(act, *(("roped", T) if part == 0 else ("q_left", (T, part - 1))))
            did(act.activation(qt[:, :, first:first + n, :], src_q.unsqueeze(2).to_broadcast([P, H, n, HD]), ACT.Copy),
                "q_part", (T, part))
            for dst in k_parts(part):
                ins = pool.tensor_copy(dst, src_k)
            if part == 2:
                did(ins, "k_split", T)
                return
            pchain(ins)
            left = rest[part]
            pool.tensor_tensor(left[:, H, :], src_k, k_parts(part)[0], ALU.subtract)
            yield
            need(pool, "q_part", (T, part))
            did(pool.tensor_tensor(left[:, 0:H, :], src_q, qt[:, :, first, :], ALU.subtract), "q_left", (T, part))
            need(pool, "q_left", (T, part))
            src_q, src_k = left[:, 0:H, :], left[:, H, :]
            yield

    def shift_v(b):
        ts = slice(b * TPB, (b + 1) * TPB)
        need(sp, "proj_v", b * TPB + TPB - 1)
        need(sp, "v_fill")
        landed(sp.dma_start(v1[WINDOW:P, ts, 0:HD], v0[0:WINDOW, ts, 0:HD]), f"v1_{b}")
        landed(sp.dma_start(v1[0:WINDOW, b * TPB + 1:(b + 1) * TPB, 0:HD],
                            v0[WINDOW:P, b * TPB:(b + 1) * TPB - 1, 0:HD]), f"v1_{b}")

    def stack(T, i):
        b, t = divmod(T, TPB)
        need(pe, "c16")
        need(pe, "q_part", (T, 2))
        need(pe, "k_split", T)
        o = bank[4][:, :].bitcast(bf16).rearrange("p (h n) -> p h n", n=P)
        if (T, i) != (0, 0):
            need(pe, "q_out", (T, 0) if i else (T - 1, 1))
        for h in range(8):
            ins = pe.transpose(o[0:SROWS, h, :], qtok[T % 2][:, 8 * i + h, :, :].rearrange("p c d -> p (c d)"), identb)
        did(ins, "q_T", (T, i))
        if i == 0:
            small_free()
            did(pe.transpose(small16[0:SROWS + MROWS, 0:P], ktok[T % 2], identb), "k_T", T)
            need(dve, "k_T", T)
            if t == 0 and b >= 2:
                need(dve, "by_key", ((b - 1) * TPB - 1, QB - 1))
            did(dve.tensor_copy(kS[0:SROWS + MROWS, b % 2, WINDOW + t * P:WINDOW + (t + 1) * P],
                                small16[0:SROWS + MROWS, 0:P]), "k_out", T)
            small_reader[0] = ("k_out", T)
        need(act, "q_T", (T, i))
        if T >= 2:
            need(act, "by_key", (T - 2, QB - 1))
        did(act.activation(qS[0:SROWS, T % 2, :, 8 * i:8 * i + 8, :],
                           o[0:SROWS].rearrange("p h (s q) -> p s h q", s=QB), ACT.Copy), "q_out", (T, i))

    def maxima(T, s):
        b, t = divmod(T, TPB)
        w = t * P + s * WINDOW
        need(pe, "k_out", T)
        need(pe, "q_out", (T, 1))
        if (T, s) != (0, 0):
            need(pe, "max", (T, s - 1) if s else (T - 1, QB - 1))
        m = k16["mask_first" if t == 0 and s == 0 else "mask"].unsqueeze(1).to_broadcast([P, 4, P])
        for e in range(2):
            pe.matmul(bank[e][:, :].rearrange("p (g n) -> p g n", g=4), identb, m, start=True, stop=False,
                      skip_group_check=True)
            for g in range(4):
                h = 2 * (4 * e + g)
                ins = pe.matmul(bank[e][:, g * P:(g + 1) * P],
                                qS[0:SROWS, T % 2, s, h:h + 2, :].rearrange("p g q -> p (g q)"),
                                kS[0:SROWS, b % 2, w:w + P], start=False, stop=True, skip_group_check=True)
            did(ins, "by_query", (T, s, e))
            need(dve, "by_query", (T, s, e))
            did(dve.tensor_reduce(maxf[T % 2][:, s * 8 + 4 * e:s * 8 + 4 * e + 4],
                                  bank[e][:, :].rearrange("p (g n) -> p g n", g=4), AX.X, ALU.max, negate=True),
                "max", (T, s) if e else (T, s, 0))

    def split_maxima(T):
        need(dve, "max", (T, QB - 1))
        if T >= 2:
            need(dve, "max_T", T - 2)
        m, f = negmax[T % 2], maxf[T % 2]
        did(dve.tensor_copy(m[:, 0, :], f), "mpart", (T, 0))
        need(dve, "mpart", (T, 0))
        did(dve.tensor_tensor(m[:, 1, :], f, m[:, 0, :], ALU.subtract), "mpart", (T, 1))

    def place_maxima(T):
        m = negmax[T % 2]
        need(pe, "mpart", (T, 1))
        small_free()
        n = MROWS * H
        did(pe.transpose(small16[0:n, 0:P], m.rearrange("p m n -> p (m n)"), identb), "max_T", T)
        need(dve, "max_T", T)
        if T >= 2:
            need(dve, f"placed{T % 2}", T - 2)
        did(dve.tensor_copy(negmaxT[T % 2][0:n, :], small16[0:n, 0:P]), "max_out", T)
        small_reader[0] = ("max_out", T)
        need(sp, "max_out", T)
        if T >= 2:
            need(sp, "by_key", (T - 2, QB - 1))
        for i in range(MROWS):
            dst = qS[SROWS + i:SROWS + i + 1, T % 2, :, :, :].rearrange("o s (g i) q -> o (s g) (i q)", i=2)
            landed(sp.dma_start(dst, negmaxT[T % 2][i * H:(i + 1) * H, :]), f"placed{T % 2}", T)

    def scores(T, s):
        b, t = divmod(T, TPB)
        n, w = QB * T + s, t * P + s * WINDOW
        need(pe, f"placed{T % 2}", T)
        m = k16["maskT_first" if t == 0 and s == 0 else "maskT"]
        for e in range(2):
            if n >= 1:
                need(pe, "exp", n - 1 if e else (n - 1, 0))
            pe.matmul(bank[2 + e][:, :], m, k16["spread"], start=True, stop=False)
            ins = pe.matmul(bank[2 + e][:, :].rearrange("p (g q) -> p g q", g=8), kS[0:SROWS + MROWS, b % 2, w:w + P],
                            qS[0:SROWS + MROWS, T % 2, s, 8 * e:8 * e + 8, :], start=False, stop=True)
            did(ins, "by_key", (T, s) if e else (T, s, 0))
            if n >= 2:
                need(act, "weighted", n - 2)
            need(act, "by_key", (T, s) if e else (T, s, 0))
            did(act.activation(probs[n % 2][:, e * 512:(e + 1) * 512], bank[2 + e][:, :], ACT.Exp), "exp",
                n if e else (n, 0))

    def weigh(T, s):
        n = QB * T + s
        need(pe, "exp", n)
        if s == 1:
            v = v0[:, T, :]
        else:
            v = v1[:, T, :]
            need(pe, f"v1_{T // TPB}")
        if s == 0 and T:
            need(pe, "o_out", T - 1)
        for j in range(4):
            ins = pe.matmul(bank[5][32 * j:32 * j + 32, s * 256:(s + 1) * 256], v,
                            probs[n % 2][:, j * 256:(j + 1) * 256], start=True, stop=True)
        did(ins, "weighted", n)

    def turn_output(T):
        need(act, "weighted", QB * T + 1)
        if T:
            need(act, "o_T", T - 1)
        did(act.activation(oT.rearrange("p g (s q) -> p s g q", s=QB),
                           bank[5][:, :].rearrange("p (s g q) -> p s g q", s=QB, g=4), ACT.Copy), "o_out", T)

    def turn_tokens(T):
        need(pe, "o_out", T)
        small_free()
        for g in range(4):
            ins = pe.transpose(small_bank[:, g * P:(g + 1) * P], oT[:, g, :], ident)
        did(ins, "o_T", T)
        need(dve, "o_T", T)
        o = small_bank[:, :].rearrange("p (j c) -> p j c", c=2 * HD)
        if T:
            need(dve, "a_T", T - 1)
        did(dve.reciprocal(rden.unsqueeze(2), o[:, :, HD:HD + 1]), "rden", T)
        need(dve, "rden", T)
        did(dve.tensor_tensor(a_tok.rearrange("p (j c) -> p j c", c=HD), o[:, :, 0:HD],
                              rden.unsqueeze(2).to_broadcast([P, H, HD]), ALU.mult), "a_tok", T)
        small_reader[0] = ("a_tok", T)

    aT_v = aT[:, :].rearrange("p (c n) -> p c n", c=NC)

    def turn_attention(T):
        need(pe, "a_tok", T)
        small_free()
        for c in range(NC):
            ins = pe.transpose(small_bank[:, c * P:(c + 1) * P], a_tok[:, c * P:(c + 1) * P], ident)
        did(ins, "a_T", T)
        need(act, "a_T", T)
        did(act.activation(aT_v[:, :, T * P:(T + 1) * P],
                           small_bank[:, 0:D].rearrange("p (c n) -> p c n", c=NC), ACT.Copy), "aT", T)
        small_reader[0] = ("aT", T)

    base = lambda T: xnT[:, :, T * P:(T + 1) * P]
    shared_readers = [None]
    GN = GT * P

    def shared_unit(n, buf, banks):
        g, k = divmod(n, FC)
        s, f0 = divmod(k * P, HS)
        hs, th, ah = buf[0], buf[1][n % 2], buf[2][n % 2]
        if n == 0:
            need(pe, "wsh", (1, S - 1))
        if shared_readers[-len(banks)]:
            need(pe, *shared_readers[-len(banks)])
        o = banks[len(shared_readers) % len(banks)]
        for i in range(2):
            for c in range(NC):
                ins = pe.matmul(o[:, i * GN:(i + 1) * GN], wsh[:, c, i, s, f0:f0 + P],
                                xnT[:, c, g * GN:(g + 1) * GN], start=c == 0, stop=c == NC - 1)
            if i == 0:
                yield
        did(ins, "shared", n)
        need(act, "shared", n)
        if n >= 2:
            need(act, "ah", n - 2)
        did(act.activation(th, o[:, 0:GN], ACT.Tanh, scale=0.5), "th", n)
        yield
        need(dve, "th", n)
        if n >= 2:
            need(dve, "hs", n - 2)
        did(dve.scalar_tensor_tensor(ah, th, 1.0, o[:, 0:GN], ALU.add, ALU.mult), "ah", n)
        need(dve, "ah", n)
        if k == 0 and g:
            need(dve, "projected", g * GT - 1)
        did(dve.scalar_tensor_tensor(hs[:, k, :], ah, 0.5, o[:, GN:2 * GN], ALU.mult, ALU.mult), "hs", n)
        shared_readers.append(("hs", n))
        yield

    def project_out(T, buf, banks):
        hs = buf[0]
        if T == 0:
            need(pe, "wo", 15 * HD)
            need(pe, "wshd")
        need(pe, "aT", T)
        need(pe, "hs", (T // GT) * FC + FC - 1)
        if shared_readers[-len(banks)]:
            need(pe, *shared_readers[-len(banks)])
        o = banks[len(shared_readers) % len(banks)]
        for c in range(NC):
            pe.matmul(o[:, 0:D], aT_v[:, c, T * P:(T + 1) * P], wo_sb[:, c, :], start=c == 0, stop=False)
        t = T % GT
        for k in range(FC):
            if k == 1:
                yield
            ins = pe.matmul(o[:, 0:D], hs[:, k, t * P:(t + 1) * P], wshd[:, k, :], start=False, stop=k == FC - 1)
        did(ins, "projected", T)
        need(act, "projected", T)
        did(act.activation(base(T), o[:, 0:D].rearrange("p (c n) -> p c n", c=NC), ACT.Copy), "base", T)
        shared_readers.append(("base", T))
        yield
        yield

    def shared_work(groups, buf, banks):
        for g in groups:
            for k in range(FC):
                yield from shared_unit(g * FC + k, buf, banks)
            for T in range(g * GT, (g + 1) * GT):
                yield from project_out(T, buf, banks)

    room = Region(wgu[:, (E - EG) * 2 * NC * F:])
    buf = (room.take(FC * GN).rearrange("p (k n) -> p k n", k=FC), [room.take(GN), room.take(GN)],
           [room.take(GN), room.take(GN)])

    def shared_first():
        yield from shared_work(range(NT // GT // 2), buf, [bank[7]])
        need(sp, "projected", NT // 2 - 1)
        for step in ("hs", "ah"):
            need(sp, step, NT // GT // 2 * FC - 1)
        yield from load_gate_up([E // EG - 1])

    def shared_second():
        need(act, "q_T", (NT - 1, 1))
        for eng in (dve, act):
            need(eng, "k_T", NT - 1)
        yield from shared_work([NT // GT // 2], late_buf, [bank[7]])

    def route():
        yield from routing()
        yield from load_down()

    rg = Region(arena[:, 0:used_words])
    NX = 6
    xg = [rg.take(D) for _ in range(NX)]
    xgT = [rg.take(D) for _ in range(2)]
    sg = [rg.take(F) for _ in range(2)]
    hh = [rg.take(2 * F).rearrange("p (i f) -> p i f", i=2) for _ in range(2)]
    hT = [rg.take(P) for _ in range(2)]
    NY = 3
    yb = [rg.take(D) for _ in range(NY)]
    late_buf = (rg.take(FC * GN).rearrange("p (k n) -> p k n", k=FC), [rg.take(GN), rg.take(GN)], [rg.take(GN), rg.take(GN)])

    def gather(i):
        if i == 0:
            need(pool, "q_T", (NT - 1, 1))
            need(pool, "q_part", (NT - 1, 2))
            need(pool, "k_T", NT - 1)
            need(pool, "route", route_n[0])
            for b in range(B):
                need(pool, f"xn{b}")
        if i >= NX:
            need(pool, "g_T", i - NX)
        landed(pool.indirect_dma_start(out=xg[i % NX], out_offset=None, in_=xn_d,
                                       in_offset=bass.IndirectOffsetOnAxis(ap=slot_token[:, i:i + 1], axis=0)),
               f"gather{i % NX}", i)

    def turn(i):
        need(pe, f"gather{i % NX}", i)
        if i >= 2:
            need(pe, "gT_out", i - 2)
        elif i == 0:
            need(pe, "max", (NT - 1, QB - 1))
        for c in range(NC):
            ins = pe.transpose(bank[i % 2][:, c * P:(c + 1) * P], xg[i % NX][:, c::NC], ident)
        did(ins, "g_T", i)
        need(dve, "g_T", i)
        if i >= 2:
            need(dve, "up", i - 2)
        did(dve.tensor_copy(xgT[i % 2], bank[i % 2][:, 0:D]), "gT_out", i)

    turning, routing_steps, shared_steps, loads = [iter(())], route(), shared_first(), load_gate_up(range(E // EG - 1))

    ROUTE = [1, 1, 1, 2]

    def turn_on():
        next(turning[0], None)

    def route_on(steps):
        for _ in range(steps):
            next(routing_steps, None)
        next(loads, None)

    def shared(pieces):
        for _ in range(pieces):
            next(shared_now[0], None)

    normalize(0)
    normalize(1)
    ahead = iter(())
    for T in range(NT):
        transpose_x(T)
        if T >= 1:
            project(T - 1)
        if T == 1:
            normalize(2)
        elif T == 5:
            normalize(3)
        elif T == 6:
            ahead = (step for r in (rotate(0), rotate(1)) for step in r)
        next(ahead, None)
    project(NT - 1)
    for _ in ahead:
        pass
    load_shared()
    for b in range(B):
        shift_v(b)
    stack(0, 0)
    stack(0, 1)
    shared_now = [shared_steps]
    for T in range(NT + 2):
        if T == NT - 1:
            for _ in shared_steps:
                pass
            shared_now[0] = shared_second()
            for i in range(NX):
                gather(i)
        turning[0] = rotate(T + 2) if T + 2 < NT else iter(())
        if T > 1:
            shared(1)
        if T < NT:
            maxima(T, 0)
        turn_on()
        if 0 < T <= NT:
            scores(T - 1, 0)
        turn_on()
        if T > 1:
            turn_tokens(T - 2)
        if T > 1:
            shared(1)
        if T < NT:
            maxima(T, 1)
            split_maxima(T)
        turn_on()
        route_on(ROUTE[0])
        if T > 1:
            turn_attention(T - 2)
        if 0 < T <= NT:
            weigh(T - 1, 0)
            scores(T - 1, 1)
        turn_on()
        if T + 1 < NT:
            stack(T + 1, 0)
        if T < NT:
            place_maxima(T)
        turn_on()
        route_on(ROUTE[1])
        if T > 1:
            shared(1)
            shared(1)
        if 0 < T <= NT:
            weigh(T - 1, 1)
        route_on(ROUTE[2])
        if T + 1 < NT:
            stack(T + 1, 1)
        turn_on()
        if 0 < T <= NT:
            turn_output(T - 1)
        route_on(ROUTE[3])
        if T:
            shared(2)
        for _ in turning[0]:
            pass
    turn(0)
    turn(1)
    for rest_of in (shared_now[0], routing_steps):
        for _ in rest_of:
            pass

    after = Region(arena[:, used_words:])
    acc = after.take(NT * D).rearrange("p (t d) -> p t d", t=NT)
    bo_sb = after.take(D)
    x_t = x.rearrange("b (t p) d -> (b t) p d", p=P)
    out_t = out.rearrange("b (t p) d -> (b t) p d", p=P)
    need(sp, "a_tok", NT - 1)
    need(sp, "q_out", (NT - 1, 1))
    landed(sp.dma_start(bo_sb, bo.partition_broadcast(P)), "bo")

    def load_acc(T):
        if T >= 4:
            need(sp, "sum", (T - 4, -2))
        landed(sp.dma_start(acc[:, T, :], x_t[T]), f"acc{T % 4}", T)

    def add_base(T):
        a = acc[:, T, :].rearrange("p (c n) -> p c n", c=NC)
        need(dve, "sum", (T, -2))
        need(dve, "base", T)
        did(dve.tensor_tensor(a, a, base(T), ALU.add), "sum", (T, -1))

    def begin_sum(T):
        if T == 0:
            need(dve, "bo")
        need(dve, f"acc{T % 4}", T)
        did(dve.tensor_tensor(acc[:, T, :], acc[:, T, :], bo_sb, ALU.add), "sum", (T, -2))
        if T < NT // 2:
            add_base(T)

    def up(i):
        if i == 0:
            need(pe, "aT", NT - 1)
            need(pe, *shared_readers[-1])
            need(pe, "wslice")
            need(pe, "exp", QB * NT - 1)
            need(pe, "wgu", (E // EG - 1, 1))
        need(pe, "gT_out", i)
        if i >= 2:
            need(pe, "h", i - 2)
        with pe.register(f"up{i}") as r:
            pe.reg_load(r, wslice[0:1, 0, i:i + 1])
            o = pe.snap(r, min_val=0, max_val=(E - 1) * 2 * NC * F)
            w = wgu[:, bass.ds(o, 2 * NC * F)].rearrange("p (g c f) -> p g c f", g=2, c=NC)
            for c in range(NC):
                ins = pe.matmul(bank[2 + i % 2][:, 0:2 * F].rearrange("p (g f) -> p g f", g=2),
                                xgT[i % 2][:, c * P:(c + 1) * P], w[:, :, c, :], start=c == 0, stop=c == NC - 1)
        did(ins, "up", i)
        need(act, "up", i)
        if i >= 2:
            need(act, "h", i - 2)
        did(act.activation(sg[i % 2], bank[2 + i % 2][:, 0:F], ACT.Silu), "silu", i)
        need(dve, "silu", i)
        if i >= 2:
            need(dve, "h_T", i - 2)
        did(dve.tensor_tensor(hh[i % 2], bank[2 + i % 2][:, F:2 * F].unsqueeze(1).to_broadcast([P, 2, F]),
                              sg[i % 2].unsqueeze(1).to_broadcast([P, 2, F]), ALU.mult), "h", i)

    def turn_h(i):
        need(pe, "h", i)
        if i >= 2:
            need(pe, "hT_out", i - 2)
        did(pe.transpose(bank[4 + i % 2][:, 0:P], hh[i % 2].rearrange("p i f -> p (i f)"), ident), "h_T", i)
        need(act, "h_T", i)
        if i >= 2:
            need(act, "down", i - 2)
        did(act.activation(hT[i % 2], bank[4 + i % 2][:, 0:P], ACT.Copy, scale=halfmask[:, i:i + 1]), "hT_out", i)

    def down(i):
        if i == 0:
            need(pe, "wdn", (E // 2 - EG, 1))
        need(pe, "hT_out", i)
        if i >= 2:
            need(pe, "y_out", i - 2)
        with pe.register(f"down{i}") as r:
            pe.reg_load(r, wslice[0:1, 1, i:i + 1])
            o = pe.snap(r, min_val=0, max_val=(E // 2 - 1) * D)
            ins = pe.matmul(bank[6 + i % 2][:, 0:D], hT[i % 2], wdn[:, bass.ds(o, D)], start=True, stop=True)
        did(ins, "down", i)
        eng = act if i % 2 else dve
        need(eng, "down", i)
        if i >= NY:
            need(eng, f"y{i % NY}", i - NY)
        if i % 2:
            did(act.activation(yb[i % NY], bank[6 + i % 2][:, 0:D], ACT.Copy), "y_out1", i)
        else:
            did(dve.tensor_copy(yb[i % NY], bank[6 + i % 2][:, 0:D]), "y_out0", i)
        at["y_out", i] = at[f"y_out{i % 2}", i]
        need(sp, f"y_out{i % 2}", i)
        landed(sp.dma_start(y_d[i * P:(i + 1) * P, :], yb[i % NY]), f"y{i % NY}", i)

    base_need = need

    def need(eng, step, item=None):
        if step == "y_out":
            step = f"y_out{item % 2}"
        base_need(eng, step, item)

    for i in range(NBLK):
        if i >= NX:
            gather(i)
        if i % 6 == 0 and i // 6 < NT:
            load_acc(i // 6)
        if i % 6 == 5 and i // 6 < NT:
            begin_sum(i // 6)
        if i >= 2:
            turn(i)
        if i >= 4:
            down(i - 4)
        if i >= 1:
            up(i - 1)
        if i >= 2:
            turn_h(i - 2)
    up(NBLK - 1)
    down(NBLK - 4)
    turn_h(NBLK - 2)
    down(NBLK - 3)
    turn_h(NBLK - 1)
    down(NBLK - 2)
    down(NBLK - 1)

    yk = wgu[:, :].rearrange("p (t k d) -> p t k d", t=NT, k=TOPK)
    late = range(NT // GT // 2 + 1, NT // GT)
    buf = late_buf

    def fetch(T):
        if T == 0:
            need(pool, "up", NBLK - 1)
            for i in range(NBLK - NY, NBLK):
                need(pool, f"y{i % NY}", i)
            need(pool, "slots")
        for k in range(TOPK):
            landed(pool.indirect_dma_start(out=yk[:, T, k, :], out_offset=None, in_=y_d,
                                           in_offset=bass.IndirectOffsetOnAxis(ap=pos_i[:, T, k:k + 1], axis=0)),
                   f"yk{T}", k)

    def sum_up(T):
        a = acc[:, T, :]
        need(dve, f"yk{T}", TOPK - 1)
        for k in range(TOPK):
            need(dve, "sum", (T, k - 1))
            did(dve.scalar_tensor_tensor(a, yk[:, T, k, :], gate[:, T, k:k + 1], a, ALU.mult, ALU.add), "sum", (T, k))
            yield
        need(sp, "sum", (T, TOPK - 1))
        landed(sp.dma_start(out_t[T], a), "out", T)

    for T in range(NT):
        fetch(T)
    shared_readers.extend([shared_readers[-1]] * 2)
    tail = shared_work(late, buf, [bank[4], bank[5], bank[0]])
    for i in (NBLK - 2, NBLK - 1):
        need(pe, "hT_out", i)
        need(pe, "gT_out", i)
    for _ in range(3 * 3):
        next(tail, None)
    for T in range(NT):
        if T >= NT // 2:
            add_base(T)
        for k, _ in enumerate(sum_up(T)):
            if k % 2:
                for _ in range(3):
                    next(tail, None)
    need(sp, "out", NT - 1)
    ctx.close()


_INS = ["x", "Wq", "Wk", "Wv", "Wo", "bo", "router_w", "router_bias", "wg", "wu", "wd", "swg", "swu", "swd"]


def kernel(**inputs):
    import concourse.bacc as bacc
    from concourse.bass_utils import run_bass_kernel_spmd

    nc = bacc.Bacc("TRN2", target_bir_lowering=False, num_devices=1)
    (w32, c32), (w16, c16) = layout_constants()
    arrays = {f"in_{n}": np.ascontiguousarray(inputs[("L0_attn_" if n in ("x", "Wq", "Wk", "Wv", "Wo", "bo") else "L0_ffn_") + n])
              for n in _INS}
    arrays["const32"], arrays["const16"] = c32, c16
    args = [nc.dram_tensor(n, a.shape, mybir.dt.from_np(a.dtype), kind="ExternalInput").ap() for n, a in arrays.items()]
    out = nc.dram_tensor("out_0", (B, L, D), mybir.dt.float32, kind="ExternalOutput").ap()
    build(nc, *args, w32, w16, out)
    r = run_bass_kernel_spmd(nc, [arrays], core_ids=[0])
    return r.results[0]["out_0"]
```

```python
from contextlib import ExitStack

import numpy as np

import concourse.bass as bass
from concourse import mybir

B, L, D = 4, 512, 256
H, HD = 16, 16
ROT = HD // 4
WINDOW = 64
ROPE_BASE = 10000.0
MASKED = -1.0e9
E, F, TOPK = 64, 64, 4
S, HS = 2, 256
P = 128
NT = B * L // P
TPB = L // P
NC = D // P
QB = P // WINDOW
NBLK = (NT * P * TOPK - E) // P + E
NQK = (H + 1) * HD
NPROJ = NQK + HD + E
FC = S * HS // P
QPARTS = (0, 0, 0, 1, 1, 2)
KPARTS = (0, 1, 2, 0, 1, 0)
SROWS = len(QPARTS) * HD
MROWS = 2
GT = 2
EPS = 1e-5
EARLY, MIDDLE = 2, 3


def layout_constants():
    pos = np.arange(L, dtype=np.float32)
    inv = np.exp(-np.log(np.float32(ROPE_BASE)) * (np.arange(0, 2 * ROT, 2).astype(np.float32) / np.float32(2 * ROT))).astype(np.float32)
    theta = (pos[:, None] * inv[None, :]).astype(np.float32)
    part = np.arange(P)
    rows = lambda a: np.ascontiguousarray(a.reshape(TPB, P, ROT).transpose(1, 0, 2).reshape(P, TPB * ROT))
    f32 = {
        "ident": np.eye(P),
        "cos": rows(np.cos(theta)),
        "sin": rows(np.sin(theta)),
        "experts": np.tile(np.arange(E), (P, 1)),
        "token": part[:, None] + P * np.arange(NT)[None, :],
        "row": part[:, None],
        "half": (part // F)[:, None],
    }
    q, j = part % WINDOW, np.arange(P)
    band = (j[None, :] > q[:, None]) & (j[None, :] <= q[:, None] + WINDOW)
    first = band & (j[None, :] >= WINDOW)
    top = (part < WINDOW)[:, None]
    cost = lambda ok: np.where(ok, 0.0, MASKED)
    b16 = {
        "identb": np.eye(P),
        "mask": cost(band),
        "mask_first": cost(first),
        "maskT": np.where(top, cost(band), 0.0),
        "maskT_first": np.where(top, cost(first), 0.0),
        "spread": np.tile(np.where(top, np.eye(P)[:, :WINDOW], 0.0), (1, H // 2)),
        "before": (part[:, None] < part[None, :]),
        "ones": np.ones((P, P)),
        "ramp": np.tile(np.arange(P), (P, 1)),
    }
    pack = lambda d: ({n: a.shape[1] for n, a in d.items()}, np.concatenate([np.asarray(a, np.float32) for a in d.values()], 1))
    w32, a32 = pack(f32)
    w16, a16 = pack(b16)
    return (w32, a32), (w16, (a16.view(np.uint32) >> 16).astype(np.uint16))


def build(nc, x, Wq, Wk, Wv, Wo, bo, router_w, router_bias, wg, wu, wd, swg, swu, swd, c32, c16, w32, w16, out):
    f32, f32r, bf16, f16 = mybir.dt.float32, mybir.dt.float32r, mybir.dt.bfloat16, mybir.dt.float16
    i32, u32 = mybir.dt.int32, mybir.dt.uint32
    ALU, ACT, AX = mybir.AluOpType, mybir.ActivationFunctionType, mybir.AxisListType
    pe, dve, act, pool, sp = nc.tensor, nc.vector, nc.scalar, nc.gpsimd, nc.sync
    ctx = ExitStack()

    sems, count, at, seen = {}, {}, {}, {}

    def did(ins, step, item=None, by=1):
        if step not in sems:
            sems[step], count[step] = ctx.enter_context(nc.semaphore("s_" + step)), 0
        ins.then_inc(sems[step], by)
        count[step] += by
        at[step, item] = count[step]
        return ins

    def need(eng, step, item=None):
        v = at[step, item]
        if seen.get((eng.engine, step), 0) < v:
            seen[eng.engine, step] = v
            eng.wait_ge(sems[step], v)

    def landed(ins, step, item=None):
        return did(ins, step, item, 16)

    def sb(name, shape, dt=f32):
        return ctx.enter_context(nc.sbuf_tensor(name, shape, dt))

    bank = [ctx.enter_context(nc.psum_tensor(f"bank{i}", [P, 512], f32)) for i in range(8)]
    cf, cb = sb("cf", [P, c32.shape[1]]), sb("cb", [P, c16.shape[1]], bf16)
    wproj = sb("wproj", [P, NC, NPROJ])
    wsh = sb("wsh", [P, NC, 2, S, HS])
    wshd = sb("wshd", [P, FC, D])
    wo_sb = sb("wo_sb", [P, NC, D])
    wgu = sb("wgu", [P, E * 2 * NC * F])
    wdn = sb("wdn", [P, E // 2 * D])
    xnT = sb("xnT", [P, NC, NT * P])
    aT = sb("aT", [P, NC * NT * P])
    qS = sb("qS", [P, 2, QB, H, WINDOW], bf16)
    kS = sb("kS", [P, 2, WINDOW + L], bf16)
    bias_sb = sb("bias_sb", [P, E])
    pos_f, pos_i = sb("pos_f", [P, NT, TOPK]), sb("pos_i", [P, NT, TOPK], i32)
    gate = sb("gate", [P, NT, TOPK])
    slot_token = sb("slot_token", [P, P], i32)
    wslice = sb("wslice", [1, 2, P], i32)
    halfmask = sb("halfmask", [P, P])
    small = sb("small", [P, 1152])
    arena = sb("arena", [P, 10500])
    xn_d = nc.dram_tensor("xn_d", (NT * P, D), f32, kind="Internal").ap()
    y_d = nc.dram_tensor("y_d", (NBLK * P, D), f32, kind="Internal").ap()

    def columns(t, widths):
        r, o = {}, 0
        for n, w in widths.items():
            r[n] = t[:, o:o + w]
            o += w
        return r

    k32, k16 = columns(cf, w32), columns(cb, w16)
    ident = k32["ident"]

    class Region:

        def __init__(self, t):
            self.t, self.o = t, 0

        def take(self, n, dt=f32):
            words = n if dt in (f32, f32r, i32, u32) else n // 2
            v = self.t[:, self.o:self.o + words]
            self.o += words
            assert self.o <= self.t.shape[1], (self.o, self.t.shape)
            return v if dt == f32 else v.bitcast(dt)

    sm = Region(small)
    stats = sm.take(TPB * 6).rearrange("p (t s) -> p t s", s=6)
    mv = sm.take(NT * 2).rearrange("p (t s) -> p t s", s=2)
    var, rstd, newt = sm.take(NT), sm.take(NT), sm.take(NT)
    top8 = sm.take(NT * 8).rearrange("p (t k) -> p t k", k=8)
    arg8 = sm.take(NT * 8, u32).rearrange("p (t k) -> p t k", k=8)
    pick = sm.take(TOPK * NT).rearrange("p (k t) -> p k t", k=TOPK)
    nblk, ends, starts, cmp = sm.take(E), sm.take(E), sm.take(E), sm.take(E)
    blk_expert, unread = sm.take(1), sm.take(1)
    slot_blk, slot_row = sm.take(NT * TOPK), sm.take(NT * TOPK)
    esum, emax = sm.take(NT), sm.take(NT)
    brow = sm.take(2 * P)

    x_b = x.rearrange("b (t p) d -> b p t d", p=P)
    xio = Region(wgu)
    x_in = [xio.take(TPB * D).rearrange("p (t d) -> p t d", d=D) for _ in range(B)]
    x_n = [xio.take(TPB * D).rearrange("p (t d) -> p t d", d=D) for _ in range(B)]
    for b in range(B):
        landed(sp.dma_start(x_in[b], x_b[b]), f"x{b}")
    rows = lambda w: w.rearrange("(p c) n -> p c n", c=NC)
    landed(act.dma_start(cf[:, :], c32), "c32")
    col = 0
    for i, (w, n) in enumerate(((Wq, H * HD), (Wk, HD), (Wv, HD), (router_w, E))):
        landed(act.dma_start(wproj[:, :, col:col + n], rows(w)), "wproj", i)
        col += n
    landed(act.dma_start(cb[:, :].bitcast(mybir.dt.uint16), c16), "c16")
    landed(act.dma_start(bias_sb[:, :], router_bias.partition_broadcast(P)), "bias")

    ar = Region(arena)
    qk = ar.take(NT * NQK).rearrange("p (t h d) -> p t h d", h=H + 1, d=HD)
    qtok = [ar.take(H * SROWS, bf16).rearrange("p (h c d) -> p h c d", h=H, d=HD) for _ in range(2)]
    used_words = ar.o
    rt = Region(wdn)
    logit = rt.take(NT * E).rearrange("p (t e) -> p t e", e=E)
    biased = rt.take(NT * E).rearrange("p (t e) -> p t e", e=E)
    v0 = ar.take(NT * 32).rearrange("p (t d) -> p t d", d=32)
    v1 = ar.take(NT * 32).rearrange("p (t d) -> p t d", d=32)
    did(pool.memset(v0[:, :, :], 1.0), "v_fill", "values")
    did(pool.memset(v1[:, :, :], 1.0), "v_fill")
    need(pool, "v_fill")
    did(pool.memset(v1[0:WINDOW, :, 0:HD], 0.0), "v_fill")

    def normalize(b):
        need(dve, f"x{b}")
        ts = slice(b * TPB, (b + 1) * TPB)
        for t in range(TPB):
            if b:
                need(dve, "moments", b * TPB + t - TPB)
            did(dve.bn_stats(stats[:, t, :], x_in[b][:, t, :]), "stats", b * TPB + t)
        for t in range(TPB):
            need(dve, "stats", b * TPB + t)
            did(dve.bn_aggr(mv[:, b * TPB + t, :], stats[:, t, :]), "moments", b * TPB + t)
        need(dve, "moments", b * TPB + TPB - 1)
        did(dve.tensor_scalar(var[:, ts], mv[:, ts, 1], EPS, None, ALU.add), "var", b)
        need(act, "var", b)
        did(act.activation(newt[:, ts], var[:, ts], ACT.Sqrt), "root", b)
        need(dve, "root", b)
        did(dve.reciprocal(rstd[:, ts], newt[:, ts]), "rs", (b, 0))
        need(dve, "rs", (b, 0))
        did(dve.tensor_tensor(newt[:, ts], rstd[:, ts], rstd[:, ts], ALU.mult), "rs", (b, 1))
        need(dve, "rs", (b, 1))
        did(dve.tensor_tensor(newt[:, ts], newt[:, ts], var[:, ts], ALU.mult), "rs", (b, 2))
        need(dve, "rs", (b, 2))
        did(dve.tensor_scalar(newt[:, ts], newt[:, ts], -0.5, 1.5, ALU.mult, ALU.add), "rs", (b, 3))
        need(dve, "rs", (b, 3))
        did(dve.tensor_tensor(rstd[:, ts], rstd[:, ts], newt[:, ts], ALU.mult), "rs", (b, 4))
        need(dve, "rs", (b, 4))
        for t in range(TPB):
            T = b * TPB + t
            did(dve.tensor_scalar(x_n[b][:, t, :], x_in[b][:, t, :], mv[:, T, 0:1], rstd[:, T:T + 1],
                                  ALU.subtract, ALU.mult), "normed", T)
        need(sp, "normed", b * TPB + TPB - 1)
        landed(sp.dma_start(xn_d[b * L:(b + 1) * L, :].rearrange("(t p) d -> p t d", p=P), x_n[b]), f"xn{b}")

    def transpose_x(T):
        b, t = divmod(T, TPB)
        need(pe, "c32")
        need(pe, "normed", T)
        if T >= 2:
            need(pe, "xT_out", T - 2)
        for c in range(NC):
            ins = pe.transpose(bank[T % 2][:, c * P:(c + 1) * P], x_n[b][:, t, c::NC], ident)
        did(ins, "x_T", T)
        need(act, "x_T", T)
        did(act.activation(xnT[:, :, T * P:(T + 1) * P], bank[T % 2][:, 0:D].rearrange("p (c n) -> p c n", c=NC),
                           ACT.Copy), "xT_out", T)

    def project(T):
        need(pe, "wproj", 3)
        need(pe, "xT_out", T)
        if T >= 4:
            need(pe, "proj_v", T - 4)
        o = bank[2 + T % 4]
        for c in range(NC):
            ins = pe.matmul(o[:, 0:NPROJ], xnT[:, c, T * P:(T + 1) * P], wproj[:, c, :],
                            start=c == 0, stop=c == NC - 1)
        did(ins, "proj", T)
        need(act, "proj", T)
        did(act.activation(qk[:, T].rearrange("p h d -> p (h d)"), o[:, 0:NQK], ACT.Copy), "proj_qk", T)
        need(dve, "proj_qk", T)
        if T == 0:
            need(dve, "v_fill")
        did(dve.tensor_copy(logit[:, T, :], o[:, NQK + HD:NPROJ]), "logit", T)
        did(dve.tensor_copy(v0[:, T, 0:HD], o[:, NQK:NQK + HD]), "proj_v", T)

    def load_shared():
        for g, w in enumerate((swg, swu)):
            for n in range(S):
                landed(sp.dma_start(wsh[:, :, g, n, :], rows(w[n])), "wsh", (g, n))
        landed(sp.dma_start(wshd[:, :, :], swd.rearrange("s (k p) d -> p (s k) d", p=P)), "wshd")
        for g in range(4):
            for j in range(4):
                r = (4 * g + j) * HD
                h = 4 * j + g
                landed(sp.dma_start(wo_sb[r % P:r % P + HD, r // P, :], Wo[h * HD:(h + 1) * HD, :]), "wo", r)

    wgu_v = wgu[:, :].rearrange("p (e c g f) -> p e c g f", e=E, g=2, c=NC)
    EG = 8

    def load_gate_up(groups):
        for b in range(B):
            need(sp, f"xn{b}")
        need(sp, "x_T", NT - 1)
        need(sp, "normed", NT - 1)
        for i in groups:
            for g, w in enumerate((wg, wu)):
                src = w[i * EG:(i + 1) * EG].rearrange("e (p c) f -> p c e f", c=NC)
                for c in range(NC):
                    landed(sp.dma_start(wgu_v[:, i * EG:(i + 1) * EG, c, g, :], src[:, c]), "wgu", (i, g, c))
                yield

    def load_down():
        wdn_v = wdn[:, :].rearrange("p (j d) -> p j d", d=D)
        need(sp, "gate")
        for j in range(0, E // 2, EG):
            for h in range(2):
                e = h * E // 2 + j
                landed(sp.dma_start(wdn_v[h * F:(h + 1) * F, j:j + EG], wd[e:e + EG].rearrange("j f d -> f j d")),
                       "wdn", (j, h))
                yield

    onehot = rt.take(TOPK * NT * E, bf16).rearrange("p (k t e) -> p k t e", k=TOPK, e=E)
    member = rt.take(NT * E, bf16).rearrange("p (t e) -> p t e", e=E)
    earlier = rt.take((NT + 1) * E, bf16).rearrange("p (t e) -> p t e", e=E)
    product = rt.take(NT * E).rearrange("p (t e) -> p t e", e=E)
    expo = biased
    table = brow[:, 0:P]
    NR = 16
    spare_rows = Region(product.rearrange("p t e -> p (t e)"))
    who = [rt.take(P, f16) for _ in range(NR // 2)] + [spare_rows.take(P, f16) for _ in range(NR // 2)]
    where = [rt.take(P, f16) for _ in range(NR // 2)] + [spare_rows.take(P, f16) for _ in range(NR // 2)]
    small_bank = bank[6]
    small16 = small_bank[:, :].bitcast(bf16)
    small_reader = [None]

    def small_free():
        if small_reader[0]:
            need(pe, *small_reader[0])

    MAGIC = float(1.5 * 2 ** 23)
    route_n = [0]

    def chain(ins):
        route_n[0] += 1
        did(ins, "route", route_n[0])
        need(dve, "route", route_n[0])

    def named(step):
        at[step, None], sems[step] = at["route", route_n[0]], sems["route"]

    over_tiles = lambda v: v.unsqueeze(1).to_broadcast([P, NT, E])
    over_k = lambda v: v.unsqueeze(2).to_broadcast([P, NT, TOPK])

    def routing():
        need(dve, "bias")
        need(dve, "c32")
        need(dve, "c16")
        need(dve, "logit", NT - 1)
        chain(dve.tensor_tensor(biased, logit, over_tiles(bias_sb[:, :]), ALU.add))
        yield
        for t in range(NT):
            ins = dve.max(top8[:, t, :], biased[:, t, :])
            if t % 8 == 7:
                chain(ins)
                yield
        for t in range(NT):
            ins = dve.max_index(arg8[:, t, :], top8[:, t, :], biased[:, t, :])
            if t % 8 == 7:
                chain(ins)
                yield
        chain(dve.tensor_copy(pick, arg8[:, :, 0:TOPK].rearrange("p t k -> p k t")))
        for k in range(TOPK):
            chain(dve.tensor_tensor(onehot[:, k], over_tiles(k32["experts"]),
                                    pick[:, k, :].unsqueeze(2).to_broadcast([P, NT, E]), ALU.is_equal))
            yield
        chain(dve.tensor_tensor(member, onehot[:, 0], onehot[:, 1], ALU.add))
        chain(dve.tensor_tensor(member, member, onehot[:, 2], ALU.add))
        yield
        chain(dve.tensor_tensor(member, member, onehot[:, 3], ALU.add))
        chain(dve.memset(earlier[:, 0, :], 0.0))
        yield
        for t in range(NT):
            chain(dve.tensor_tensor(earlier[:, t + 1, :], earlier[:, t, :], member[:, t, :], ALU.add))
            if t % 4 == 3:
                yield
        named("earlier")
        yield
        need(pe, "c16")
        need(pe, "earlier")
        small_free()
        total = small_bank[:, 0:E]
        did(pe.matmul(total, k16["ones"], earlier[:, NT, :], start=True, stop=True), "totals")
        need(dve, "totals")
        chain(dve.tensor_scalar(nblk, total, 1.0 / P, 0.5 - 1.0 / (2 * P), ALU.mult, ALU.add))
        named("totals_read")
        small_reader[0] = ("totals_read", None)
        chain(dve.tensor_scalar(nblk, nblk, MAGIC, None, ALU.add))
        chain(dve.tensor_scalar(nblk, nblk, MAGIC, None, ALU.subtract))
        chain(dve.memset(cmp, 1.0))
        chain(dve.tensor_tensor_scan(ends, cmp, nblk, 0.0, ALU.mult, ALU.add))
        chain(dve.tensor_tensor(starts, ends, nblk, ALU.subtract))
        chain(dve.tensor_scalar(starts, starts, float(P), None, ALU.mult))
        yield
        for i in range(2):
            small_free()
            ranks = small_bank[:, :].rearrange("p (t e) -> p t e", e=E)
            for t in range(8 * i, 8 * i + 8):
                pe.matmul(ranks[:, t % 8, :], k16["before"], member[:, t, :], start=True, stop=False)
                ins = pe.matmul(ranks[:, t % 8, :], k16["ones"], earlier[:, t, :], start=False, stop=True)
            did(ins, "ranked", i)
            need(dve, "ranked", i)
            chain(dve.tensor_tensor(biased[:, 8 * i:8 * i + 8, :], ranks,
                                    starts.unsqueeze(1).to_broadcast([P, 8, E]), ALU.add))
            at["rank_read", i], sems["rank_read"] = at["route", route_n[0]], sems["route"]
            small_reader[0] = ("rank_read", i)
            yield
        for k in range(TOPK):
            chain(dve.tensor_tensor(product, onehot[:, k], biased, ALU.mult))
            yield
            chain(dve.tensor_reduce(pos_f[:, :, k], product, AX.X, ALU.add))
            yield
        flat_pos = pos_f[:, :, :].rearrange("p t k -> p (t k)")
        chain(dve.tensor_scalar(slot_blk, flat_pos, 1.0 / P, -(0.5 - 1.0 / (2 * P)), ALU.mult, ALU.add))
        chain(dve.tensor_scalar(slot_blk, slot_blk, MAGIC, None, ALU.add))
        chain(dve.tensor_scalar(slot_blk, slot_blk, MAGIC, None, ALU.subtract))
        chain(dve.scalar_tensor_tensor(slot_row, slot_blk, -float(P), flat_pos, ALU.mult, ALU.add))
        need(pool, "route", route_n[0])
        GR = 8
        for i0 in range(0, NT * TOPK + GR, GR):
            for i in range(i0, i0 + GR if i0 < NT * TOPK else i0):
                if i >= NR:
                    need(dve, "tabled", i0 - NR)
                    need(pool, "tabled", i0 - NR)
                eng, step = ((pool, "where"), (dve, "who"))[i % 2]
                did(eng.tensor_scalar(where[i % NR], k16["ramp"], slot_row[:, i:i + 1], None, ALU.is_equal), step, ("where", i))
                did(dve.tensor_scalar(who[i % NR], k16["ramp"], slot_blk[:, i:i + 1],
                                      k32["token"][:, i // TOPK:i // TOPK + 1], ALU.is_equal, ALU.mult), "who", i)
                if i % 2:
                    yield
            j0 = i0 - GR
            if j0 < 0:
                continue
            small_free()
            for j in range(j0, j0 + GR):
                if j % 2 == 0:
                    need(pe, "where", ("where", j))
                need(pe, "who", j)
                ins = pe.matmul(small_bank[:, 0:P], where[j % NR], who[j % NR], start=j == j0, stop=j == j0 + GR - 1)
            did(ins, "tabled", j0)
            need(dve, "tabled", j0)
            if j0 == 0:
                chain(dve.tensor_copy(table, small_bank[:, 0:P]))
            else:
                chain(dve.tensor_tensor(table, table, small_bank[:, 0:P], ALU.add))
            named(f"table_read{j0}")
            small_reader[0] = (f"table_read{j0}", None)
        chain(dve.tensor_copy(slot_token[:, :], table))
        named("slot_token")
        did(dve.tensor_copy(pos_i[:, :, :], pos_f[:, :, :]), "slots")
        yield
        chain(dve.tensor_scalar(cmp, ends, k32["row"], None, ALU.is_le))
        chain(dve.tensor_reduce(blk_expert, cmp, AX.X, ALU.add))
        chain(dve.tensor_scalar(blk_expert, blk_expert, float(E - 1), None, ALU.min))
        diag, onesf = brow[:, 0:P], brow[:, P:2 * P]
        chain(dve.tensor_scalar(diag, ident, blk_expert, None, ALU.mult))
        chain(dve.memset(onesf, 1.0))
        named("diag")
        yield
        small_free()
        need(pe, "diag")
        expert_row = small_bank[:, 0:P]
        did(pe.matmul(expert_row, onesf, diag, start=True, stop=True), "expert_row")
        need(dve, "expert_row")
        chain(dve.tensor_scalar(diag, expert_row, float(E // 2), None, ALU.is_ge))
        chain(dve.tensor_scalar(halfmask[:, :], diag, k32["half"], None, ALU.is_equal))
        chain(dve.scalar_tensor_tensor(onesf, diag, -float(E // 2), expert_row, ALU.mult, ALU.add))
        chain(dve.tensor_scalar(wslice[0:1, 0, :], expert_row[0:1, :], 2.0 * NC * F, None, ALU.mult))
        chain(dve.tensor_scalar(wslice[0:1, 1, :], onesf[0:1, :], float(D), None, ALU.mult))
        named("wslice")
        small_reader[0] = ("wslice", None)
        yield
        chain(dve.tensor_reduce(emax, logit, AX.X, ALU.max))
        chain(dve.tensor_tensor(expo, logit, emax.unsqueeze(2).to_broadcast([P, NT, E]), ALU.subtract))
        named("shifted")
        yield
        need(act, "shifted")
        did(act.activation(expo, expo, ACT.Exp), "expo")
        yield
        need(dve, "expo")
        chain(dve.tensor_reduce(esum, expo, AX.X, ALU.add))
        chain(dve.reciprocal(esum, esum))
        yield
        for k in range(TOPK):
            chain(dve.tensor_tensor(product, onehot[:, k], expo, ALU.mult))
            yield
            chain(dve.tensor_reduce(gate[:, :, k], product, AX.X, ALU.add))
            yield
        chain(dve.tensor_tensor(gate[:, :, :], gate[:, :, :], over_k(esum), ALU.mult))
        chain(dve.tensor_reduce(emax, gate[:, :, :], AX.X, ALU.add))
        chain(dve.reciprocal(emax, emax))
        did(dve.tensor_tensor(gate[:, :, :], gate[:, :, :], over_k(emax), ALU.mult), "gate")

    ktok = [ar.take(SROWS + MROWS, bf16) for _ in range(2)]
    probs = [ar.take(H * WINDOW) for _ in range(2)]
    oT = ar.take(4 * P).rearrange("p (g n) -> p g n", g=4)
    rope = [ar.take((H + 1) * ROT).rearrange("p (h d) -> p h d", d=ROT) for _ in range(4)]
    rest = [ar.take((H + 1) * HD).rearrange("p (h d) -> p h d", d=HD) for _ in range(2)]
    spent = Region(wproj[:, :, :].rearrange("p c n -> p (c n)"))
    a_tok = spent.take(D)
    maxf = [spent.take(H) for _ in range(2)]
    maxrest = spent.take(H)
    negmax = [spent.take(MROWS * H, bf16).rearrange("p (m n) -> p m n", m=MROWS) for _ in range(2)]
    negmaxT = [spent.take(P, bf16) for _ in range(2)]
    rden = spent.take(H)
    for i in range(2):
        did(pool.memset(ktok[i][:, :], 1.0), "fill", ("k", i))
        did(pool.memset(kS[:, i, 0:WINDOW], 0.0), "fill", ("kS", i))
    need(pool, "fill", ("kS", 1))
    identb = k16["identb"]
    pool_n = [0]

    def pchain(ins):
        pool_n[0] += 1
        did(ins, "prep", pool_n[0])
        need(pool, "prep", pool_n[0])

    def rotate(T):
        t = T % TPB
        need(pool, "c32")
        need(pool, "proj_qk", T)
        x1, x2 = qk[:, T, :, 0:ROT], qk[:, T, :, ROT:2 * ROT]
        cs = k32["cos"][:, t * ROT:(t + 1) * ROT].unsqueeze(1).to_broadcast([P, H + 1, ROT])
        sn = k32["sin"][:, t * ROT:(t + 1) * ROT].unsqueeze(1).to_broadcast([P, H + 1, ROT])
        if T:
            need(pool, "k_split", T - 1)
        pool.tensor_tensor(rope[0], x1, cs, ALU.mult)
        pool.tensor_tensor(rope[1], x2, sn, ALU.mult)
        pool.tensor_tensor(rope[2], x1, sn, ALU.mult)
        pchain(pool.tensor_tensor(rope[3], x2, cs, ALU.mult))
        pool.tensor_tensor(x1, rope[0], rope[1], ALU.subtract)
        pchain(pool.tensor_tensor(x2, rope[2], rope[3], ALU.add))
        at["roped", T], sems["roped"] = at["prep", pool_n[0]], sems["prep"]
        yield
        q, k = qk[:, T, 0:H, :], qk[:, T, H, :]
        qt, kt = qtok[T % 2], ktok[T % 2]
        if T >= 2:
            need(pool, "k_T", T - 2)
            need(act, "q_T", (T - 2, 1))
        pchain(pool.tensor_scalar(k, k, HD ** -0.5, None, ALU.mult))
        k_parts = lambda part: [kt[:, i * HD:(i + 1) * HD] for i, x in enumerate(KPARTS) if x == part]
        src_q, src_k = q, k
        for part in range(3):
            n = QPARTS.count(part)
            first = QPARTS.index(part)
            need(act, *(("roped", T) if part == 0 else ("q_left", (T, part - 1))))
            did(act.activation(qt[:, :, first:first + n, :], src_q.unsqueeze(2).to_broadcast([P, H, n, HD]), ACT.Copy),
                "q_part", (T, part))
            for dst in k_parts(part):
                ins = pool.tensor_copy(dst, src_k)
            if part == 2:
                did(ins, "k_split", T)
                return
            pchain(ins)
            left = rest[part]
            pool.tensor_tensor(left[:, H, :], src_k, k_parts(part)[0], ALU.subtract)
            yield
            need(pool, "q_part", (T, part))
            did(pool.tensor_tensor(left[:, 0:H, :], src_q, qt[:, :, first, :], ALU.subtract), "q_left", (T, part))
            need(pool, "q_left", (T, part))
            src_q, src_k = left[:, 0:H, :], left[:, H, :]
            yield

    def shift_v(b):
        ts = slice(b * TPB, (b + 1) * TPB)
        need(sp, "proj_v", b * TPB + TPB - 1)
        need(sp, "v_fill")
        landed(sp.dma_start(v1[WINDOW:P, ts, 0:HD], v0[0:WINDOW, ts, 0:HD]), f"v1_{b}")
        landed(sp.dma_start(v1[0:WINDOW, b * TPB + 1:(b + 1) * TPB, 0:HD],
                            v0[WINDOW:P, b * TPB:(b + 1) * TPB - 1, 0:HD]), f"v1_{b}")

    def stack(T, i):
        b, t = divmod(T, TPB)
        need(pe, "c16")
        need(pe, "q_part", (T, 2))
        need(pe, "k_split", T)
        o = bank[4][:, :].bitcast(bf16).rearrange("p (h n) -> p h n", n=P)
        if (T, i) != (0, 0):
            need(pe, "q_out", (T, 0) if i else (T - 1, 1))
        for h in range(8):
            ins = pe.transpose(o[0:SROWS, h, :], qtok[T % 2][:, 8 * i + h, :, :].rearrange("p c d -> p (c d)"), identb)
        did(ins, "q_T", (T, i))
        if i == 0:
            small_free()
            did(pe.transpose(small16[0:SROWS + MROWS, 0:P], ktok[T % 2], identb), "k_T", T)
            need(dve, "k_T", T)
            if t == 0 and b >= 2:
                need(dve, "by_key", ((b - 1) * TPB - 1, QB - 1))
            did(dve.tensor_copy(kS[0:SROWS + MROWS, b % 2, WINDOW + t * P:WINDOW + (t + 1) * P],
                                small16[0:SROWS + MROWS, 0:P]), "k_out", T)
            small_reader[0] = ("k_out", T)
        need(act, "q_T", (T, i))
        if T >= 2:
            need(act, "by_key", (T - 2, QB - 1))
        did(act.activation(qS[0:SROWS, T % 2, :, 8 * i:8 * i + 8, :],
                           o[0:SROWS].rearrange("p h (s q) -> p s h q", s=QB), ACT.Copy), "q_out", (T, i))

    def maxima(T, s):
        b, t = divmod(T, TPB)
        w = t * P + s * WINDOW
        need(pe, "k_out", T)
        need(pe, "q_out", (T, 1))
        if (T, s) != (0, 0):
            need(pe, "max", (T, s - 1) if s else (T - 1, QB - 1))
        m = k16["mask_first" if t == 0 and s == 0 else "mask"].unsqueeze(1).to_broadcast([P, 4, P])
        for e in range(2):
            pe.matmul(bank[e][:, :].rearrange("p (g n) -> p g n", g=4), identb, m, start=True, stop=False,
                      skip_group_check=True)
            for g in range(4):
                h = 2 * (4 * e + g)
                ins = pe.matmul(bank[e][:, g * P:(g + 1) * P],
                                qS[0:SROWS, T % 2, s, h:h + 2, :].rearrange("p g q -> p (g q)"),
                                kS[0:SROWS, b % 2, w:w + P], start=False, stop=True, skip_group_check=True)
            did(ins, "by_query", (T, s, e))
            need(dve, "by_query", (T, s, e))
            did(dve.tensor_reduce(maxf[T % 2][:, s * 8 + 4 * e:s * 8 + 4 * e + 4],
                                  bank[e][:, :].rearrange("p (g n) -> p g n", g=4), AX.X, ALU.max, negate=True),
                "max", (T, s) if e else (T, s, 0))

    def split_maxima(T):
        need(dve, "max", (T, QB - 1))
        if T >= 2:
            need(dve, "max_T", T - 2)
        m, f = negmax[T % 2], maxf[T % 2]
        did(dve.tensor_copy(m[:, 0, :], f), "mpart", (T, 0))
        need(dve, "mpart", (T, 0))
        did(dve.tensor_tensor(m[:, 1, :], f, m[:, 0, :], ALU.subtract), "mpart", (T, 1))

    def place_maxima(T):
        m = negmax[T % 2]
        need(pe, "mpart", (T, 1))
        small_free()
        n = MROWS * H
        did(pe.transpose(small16[0:n, 0:P], m.rearrange("p m n -> p (m n)"), identb), "max_T", T)
        need(dve, "max_T", T)
        if T >= 2:
            need(dve, f"placed{T % 2}", T - 2)
        did(dve.tensor_copy(negmaxT[T % 2][0:n, :], small16[0:n, 0:P]), "max_out", T)
        small_reader[0] = ("max_out", T)
        need(sp, "max_out", T)
        if T >= 2:
            need(sp, "by_key", (T - 2, QB - 1))
        for i in range(MROWS):
            dst = qS[SROWS + i:SROWS + i + 1, T % 2, :, :, :].rearrange("o s (g i) q -> o (s g) (i q)", i=2)
            landed(sp.dma_start(dst, negmaxT[T % 2][i * H:(i + 1) * H, :]), f"placed{T % 2}", T)

    def scores(T, s):
        b, t = divmod(T, TPB)
        n, w = QB * T + s, t * P + s * WINDOW
        need(pe, f"placed{T % 2}", T)
        m = k16["maskT_first" if t == 0 and s == 0 else "maskT"]
        for e in range(2):
            if n >= 1:
                need(pe, "exp", n - 1 if e else (n - 1, 0))
            pe.matmul(bank[2 + e][:, :], m, k16["spread"], start=True, stop=False)
            ins = pe.matmul(bank[2 + e][:, :].rearrange("p (g q) -> p g q", g=8), kS[0:SROWS + MROWS, b % 2, w:w + P],
                            qS[0:SROWS + MROWS, T % 2, s, 8 * e:8 * e + 8, :], start=False, stop=True)
            did(ins, "by_key", (T, s) if e else (T, s, 0))
            if n >= 2:
                need(act, "weighted", n - 2)
            need(act, "by_key", (T, s) if e else (T, s, 0))
            did(act.activation(probs[n % 2][:, e * 512:(e + 1) * 512], bank[2 + e][:, :], ACT.Exp), "exp",
                n if e else (n, 0))

    def weigh(T, s):
        n = QB * T + s
        need(pe, "exp", n)
        if s == 1:
            v = v0[:, T, :]
        else:
            v = v1[:, T, :]
            need(pe, f"v1_{T // TPB}")
        if s == 0 and T:
            need(pe, "o_out", T - 1)
        for j in range(4):
            ins = pe.matmul(bank[5][32 * j:32 * j + 32, s * 256:(s + 1) * 256], v,
                            probs[n % 2][:, j * 256:(j + 1) * 256], start=True, stop=True)
        did(ins, "weighted", n)

    def turn_output(T):
        need(act, "weighted", QB * T + 1)
        if T:
            need(act, "o_T", T - 1)
        did(act.activation(oT.rearrange("p g (s q) -> p s g q", s=QB),
                           bank[5][:, :].rearrange("p (s g q) -> p s g q", s=QB, g=4), ACT.Copy), "o_out", T)

    def turn_tokens(T):
        need(pe, "o_out", T)
        small_free()
        for g in range(4):
            ins = pe.transpose(small_bank[:, g * P:(g + 1) * P], oT[:, g, :], ident)
        did(ins, "o_T", T)
        need(dve, "o_T", T)
        o = small_bank[:, :].rearrange("p (j c) -> p j c", c=2 * HD)
        if T:
            need(dve, "a_T", T - 1)
        did(dve.reciprocal(rden.unsqueeze(2), o[:, :, HD:HD + 1]), "rden", T)
        need(dve, "rden", T)
        did(dve.tensor_tensor(a_tok.rearrange("p (j c) -> p j c", c=HD), o[:, :, 0:HD],
                              rden.unsqueeze(2).to_broadcast([P, H, HD]), ALU.mult), "a_tok", T)
        small_reader[0] = ("a_tok", T)

    aT_v = aT[:, :].rearrange("p (c n) -> p c n", c=NC)

    def turn_attention(T):
        need(pe, "a_tok", T)
        small_free()
        for c in range(NC):
            ins = pe.transpose(small_bank[:, c * P:(c + 1) * P], a_tok[:, c * P:(c + 1) * P], ident)
        did(ins, "a_T", T)
        need(act, "a_T", T)
        did(act.activation(aT_v[:, :, T * P:(T + 1) * P],
                           small_bank[:, 0:D].rearrange("p (c n) -> p c n", c=NC), ACT.Copy), "aT", T)
        small_reader[0] = ("aT", T)

    base = lambda T: xnT[:, :, T * P:(T + 1) * P]
    shared_readers = [None]
    GN = GT * P

    def shared_unit(n, buf, banks):
        g, k = divmod(n, FC)
        s, f0 = divmod(k * P, HS)
        hs, th, ah = buf[0], buf[1][n % 2], buf[2][n % 2]
        if n == 0:
            need(pe, "wsh", (1, S - 1))
        if shared_readers[-len(banks)]:
            need(pe, *shared_readers[-len(banks)])
        o = banks[len(shared_readers) % len(banks)]
        for i in range(2):
            for c in range(NC):
                ins = pe.matmul(o[:, i * GN:(i + 1) * GN], wsh[:, c, i, s, f0:f0 + P],
                                xnT[:, c, g * GN:(g + 1) * GN], start=c == 0, stop=c == NC - 1)
            if i == 0:
                yield
        did(ins, "shared", n)
        need(act, "shared", n)
        if n >= 2:
            need(act, "ah", n - 2)
        did(act.activation(th, o[:, 0:GN], ACT.Tanh, scale=0.5), "th", n)
        yield
        need(dve, "th", n)
        if n >= 2:
            need(dve, "hs", n - 2)
        did(dve.scalar_tensor_tensor(ah, th, 1.0, o[:, 0:GN], ALU.add, ALU.mult), "ah", n)
        need(dve, "ah", n)
        if k == 0 and g:
            need(dve, "projected", g * GT - 1)
        did(dve.scalar_tensor_tensor(hs[:, k, :], ah, 0.5, o[:, GN:2 * GN], ALU.mult, ALU.mult), "hs", n)
        shared_readers.append(("hs", n))
        yield

    def project_out(T, buf, banks):
        hs = buf[0]
        if T == 0:
            need(pe, "wo", 15 * HD)
            need(pe, "wshd")
        need(pe, "aT", T)
        need(pe, "hs", (T // GT) * FC + FC - 1)
        if shared_readers[-len(banks)]:
            need(pe, *shared_readers[-len(banks)])
        o = banks[len(shared_readers) % len(banks)]
        for c in range(NC):
            pe.matmul(o[:, 0:D], aT_v[:, c, T * P:(T + 1) * P], wo_sb[:, c, :], start=c == 0, stop=False)
        t = T % GT
        for k in range(FC):
            if k == 1:
                yield
            ins = pe.matmul(o[:, 0:D], hs[:, k, t * P:(t + 1) * P], wshd[:, k, :], start=False, stop=k == FC - 1)
        did(ins, "projected", T)
        need(act, "projected", T)
        did(act.activation(base(T), o[:, 0:D].rearrange("p (c n) -> p c n", c=NC), ACT.Copy), "base", T)
        shared_readers.append(("base", T))
        yield
        yield

    def shared_work(groups, buf, banks):
        for g in groups:
            for k in range(FC):
                yield from shared_unit(g * FC + k, buf, banks)
            for T in range(g * GT, (g + 1) * GT):
                yield from project_out(T, buf, banks)

    room = Region(wgu[:, (E - EG) * 2 * NC * F:])
    buf = (room.take(FC * GN).rearrange("p (k n) -> p k n", k=FC), [room.take(GN), room.take(GN)],
           [room.take(GN), room.take(GN)])

    def shared_first():
        yield from shared_work(range(EARLY), buf, [bank[7]])
        need(sp, "projected", EARLY * GT - 1)
        for step in ("hs", "ah"):
            need(sp, step, EARLY * FC - 1)
        yield from load_gate_up([E // EG - 1])

    def shared_second():
        for eng in (dve, act):
            need(eng, "q_T", (NT - 1, 1))
            need(eng, "k_T", NT - 1)
        yield from shared_work(range(EARLY, MIDDLE), late_buf, [bank[7]])

    def route():
        yield from routing()
        yield from load_down()

    rg = Region(arena[:, 0:used_words])
    NX, NB, NY = 7, 3, 3
    xg = [rg.take(D) for _ in range(NX)]
    xgT = [rg.take(D) for _ in range(NB)]
    wcur = [rg.take(2 * NC * F) for _ in range(NB)]
    hT = [rg.take(P) for _ in range(NB)]
    small_at = rg.o
    sg = [rg.take(P) for _ in range(NB)]
    yb = [rg.take(D) for _ in range(NY)]
    late_small = Region(arena[:, small_at:small_at + 4 * GN])
    late_buf = (rg.take(FC * GN).rearrange("p (k n) -> p k n", k=FC), [late_small.take(GN) for _ in range(2)],
                [late_small.take(GN) for _ in range(2)])

    def gather(i):
        if i == 0:
            need(pool, "q_T", (NT - 1, 1))
            need(pool, "q_part", (NT - 1, 2))
            need(pool, "k_T", NT - 1)
            need(pool, "slot_token")
            for b in range(B):
                need(pool, f"xn{b}")
        if i >= NX:
            need(pool, "g_T", i - NX)
        landed(pool.indirect_dma_start(out=xg[i % NX], out_offset=None, in_=xn_d,
                                       in_offset=bass.IndirectOffsetOnAxis(ap=slot_token[:, i:i + 1], axis=0)),
               f"gather{i % NX}", i)

    turn_bank = (bank[0], bank[1], bank[5])

    def turn(i):
        need(pe, f"gather{i % NX}", i)
        if i >= NB:
            need(pe, "gT_out", i - NB)
        elif i == 0:
            need(pe, "max", (NT - 1, QB - 1))
        for c in range(NC):
            ins = pe.transpose(turn_bank[i % NB][:, c * P:(c + 1) * P], xg[i % NX][:, c::NC], ident)
        did(ins, "g_T", i)
        need(dve, "g_T", i)
        if i >= NB:
            need(dve, "up", i - NB)
        did(dve.tensor_copy(xgT[i % NB], turn_bank[i % NB][:, 0:D]), "gT_out", i)

    turning, routing_steps, shared_steps, loads = [iter(())], route(), shared_first(), load_gate_up(range(E // EG - 1))

    need(act, "v_fill", "values")
    act.activation(unread, v0[:, 0, 0:1], ACT.Sqrt)
    normalize(0)
    ahead = iter(())
    for T in range(NT):
        transpose_x(T)
        if T == 1:
            normalize(1)
        if T >= 1:
            project(T - 1)
        if T == 1:
            normalize(2)
        elif T == 5:
            normalize(3)
        if T == 5:
            ahead = (step for r in (rotate(0), rotate(1)) for step in r)
        next(ahead, None)
    project(NT - 1)
    for _ in ahead:
        pass
    load_shared()
    for b in range(B):
        shift_v(b)
    need(pe, "proj_v", NT - 1)
    stack(0, 0)
    stack(0, 1)
    shared_now = [shared_steps]
    this = lambda f, *i: lambda T: f(T, *i) if T < NT else None
    following = lambda f, *i: lambda T: f(T + 1, *i) if T + 1 < NT else None
    last = lambda f, *i: lambda T: f(T - 1, *i) if 0 < T <= NT else None
    old = lambda f, *i: lambda T: f(T - 2, *i) if T > 1 else None
    steps = {
        "maxima0": this(maxima, 0), "maxima1": this(maxima, 1), "split": this(split_maxima), "place": this(place_maxima),
        "stack0": following(stack, 0), "stack1": following(stack, 1),
        "scores0": last(scores, 0), "scores1": last(scores, 1), "weigh0": last(weigh, 0), "weigh1": last(weigh, 1),
        "output": last(turn_output), "tokens": old(turn_tokens), "attention": old(turn_attention),
        "begin": lambda T: begun.append(T) if T == 1 else None,
        "shared": lambda T: next(shared_now[0], None) if begun else None,
        "turn": lambda T: next(turning[0], None),
        "route": lambda T: next(routing_steps, None),
        "load": lambda T: next(loads, None),
    }
    begun = []
    ORDER = ("turn maxima0 turn tokens shared scores0 maxima1 attention turn route shared turn scores1 split "
             "stack0 weigh0 load load turn route shared load place shared weigh1 turn route stack1 begin "
             "output load shared route shared route").split()
    for T in range(NT + 2):
        if T == NT - 1:
            for _ in shared_steps:
                pass
            shared_now[0] = shared_second()
            for i in range(NX):
                gather(i)
        turning[0] = rotate(T + 2) if T + 2 < NT else iter(())
        for step in ORDER:
            steps[step](T)
        for _ in turning[0]:
            pass
    turn(0)
    turn(1)
    for rest_of in (shared_now[0], routing_steps):
        for _ in rest_of:
            pass

    after = Region(arena[:, used_words:])
    acc = after.take(NT * D).rearrange("p (t d) -> p t d", t=NT)
    bo_sb = after.take(D)
    x_t = x.rearrange("b (t p) d -> (b t) p d", p=P)
    out_t = out.rearrange("b (t p) d -> (b t) p d", p=P)
    need(sp, "a_tok", NT - 1)
    need(sp, "q_out", (NT - 1, 1))
    landed(sp.dma_start(bo_sb, bo.partition_broadcast(P)), "bo")

    def load_acc(T):
        if T >= 4:
            need(sp, "sum", (T - 4, 1))
        landed(sp.dma_start(acc[:, T, :], x_t[T]), f"acc{T % 4}", T)

    sum_n = [0] * NT

    def add(T, f, *operands):
        if sum_n[T]:
            need(dve, "sum", (T, sum_n[T]))
        sum_n[T] += 1
        did(f(*operands), "sum", (T, sum_n[T]))

    def add_base(T):
        a = acc[:, T, :].rearrange("p (c n) -> p c n", c=NC)
        need(dve, "base", T)
        add(T, dve.tensor_tensor, a, a, base(T), ALU.add)

    def begin_sum(T):
        if T == 0:
            need(dve, "bo")
        need(dve, f"acc{T % 4}", T)
        add(T, dve.tensor_tensor, acc[:, T, :], acc[:, T, :], bo_sb, ALU.add)

    def pick_weights(i):
        if i == 0:
            need(act, "wslice")
            need(act, "wgu", (E // EG - 1, 1, NC - 1))
            need(act, "q_T", (NT - 1, 1))
            need(act, "k_T", NT - 1)
        if i >= NB:
            need(act, "up", i - NB)
        with act.register(f"expert{i}") as r:
            act.reg_load(r, wslice[0:1, 0, i:i + 1])
            o = act.snap(r, min_val=0, max_val=(E - 1) * 2 * NC * F)
            did(act.activation(wcur[i % NB], wgu[:, bass.ds(o, 2 * NC * F)], ACT.Copy), "weights", i)

    def up(i):
        if i == 0:
            need(pe, "aT", NT - 1)
            need(pe, *shared_readers[-1])
            need(pe, "wslice")
            need(pe, "exp", QB * NT - 1)
        need(pe, "gT_out", i)
        if i >= NB:
            need(pe, "h", i - NB)
        need(pe, "weights", i)
        for c in range(NC):
            ins = pe.matmul(bank[2 + i % NB][:, 0:P], wcur[i % NB][:, c * 2 * F:(c + 1) * 2 * F],
                            xgT[i % NB][:, c * P:(c + 1) * P], start=c == 0, stop=c == NC - 1)
        did(ins, "up", i)
        g, u = bank[2 + i % NB][0:F, 0:P], bank[2 + i % NB][F:P, 0:P]
        need(act, "up", i)
        if i >= NB:
            need(act, "h", i - NB)
        for half in (slice(0, F), slice(F, P)):
            ins = act.activation(sg[i % NB][half], g, ACT.Silu)
        did(ins, "silu", i)
        need(dve, "silu", i)
        if i >= NB:
            need(dve, "down", i - NB)
        for half in (slice(0, F), slice(F, P)):
            ins = dve.scalar_tensor_tensor(hT[i % NB][half], u, halfmask[half, i:i + 1], sg[i % NB][half], ALU.mult, ALU.mult)
        did(ins, "h", i)

    down_reg = [ctx.enter_context(pe.register(f"down{i}")) for i in range(2)]

    def find_down(i):
        if i == 0:
            need(pe, "wslice")
        pe.reg_load(down_reg[i % 2], wslice[0:1, 1, i:i + 1])

    def down(i):
        if i == 0:
            need(pe, "wdn", (E // 2 - EG, 1))
        need(pe, "h", i)
        if i >= 2:
            need(pe, "y_out", i - 2)
        o = pe.snap(down_reg[i % 2], min_val=0, max_val=(E // 2 - 1) * D)
        ins = pe.matmul(bank[6 + i % 2][:, 0:D], hT[i % NB], wdn[:, bass.ds(o, D)], start=True, stop=True)
        did(ins, "down", i)
        need(act, "down", i)
        if i >= NY:
            need(act, f"y{i % NY}", i - NY)
        did(act.activation(yb[i % NY], bank[6 + i % 2][:, 0:D], ACT.Copy), "y_out", i)
        need(sp, "y_out", i)
        landed(sp.dma_start(y_d[i * P:(i + 1) * P, :], yb[i % NY]), f"y{i % NY}", i)

    BPT = 4
    pick_weights(0)
    for i in range(NBLK):
        if i >= NX:
            gather(i)
        T, part = divmod(i, BPT)
        if part == 0 and T < NT:
            load_acc(T)
        if part == BPT // 2 and T < NT:
            begin_sum(T)
        if part == BPT - 1 and T < MIDDLE * GT:
            add_base(T)
        if i >= 2:
            turn(i)
        if i >= 4:
            down(i - 4)
        if i >= 3:
            find_down(i - 3)
        if i >= 1:
            up(i - 1)
        if i + 1 < NBLK:
            pick_weights(i + 1)
    down(NBLK - 4)
    find_down(NBLK - 3)
    up(NBLK - 1)
    down(NBLK - 3)
    find_down(NBLK - 2)
    down(NBLK - 2)
    find_down(NBLK - 1)
    down(NBLK - 1)

    yk = wgu[:, :].rearrange("p (t k d) -> p t k d", t=NT, k=TOPK)
    AHEAD = 6

    def fetched(T, k):
        return (f"yk{T}_{k}", None) if T == NT - 1 else (f"yk{T}", TOPK - 1)

    def fetch(T):
        if T == 0:
            need(pool, "weights", NBLK - 1)
            for i in range(NBLK - NY, NBLK):
                need(pool, f"y{i % NY}", i)
            need(pool, "slots")
        for k in range(TOPK):
            landed(pool.indirect_dma_start(out=yk[:, T, k, :], out_offset=None, in_=y_d,
                                           in_offset=bass.IndirectOffsetOnAxis(ap=pos_i[:, T, k:k + 1], axis=0)),
                   *fetched(T, k))

    def sum_up(T):
        a = acc[:, T, :]
        base_first = T >= NT - 2
        if T >= MIDDLE * GT and base_first:
            add_base(T)
        for k in range(TOPK):
            need(dve, *fetched(T, k))
            add(T, dve.scalar_tensor_tensor, a, yk[:, T, k, :], gate[:, T, k:k + 1], a, ALU.mult, ALU.add)
            yield k
        if T >= MIDDLE * GT and not base_first:
            add_base(T)
        need(sp, "sum", (T, sum_n[T]))
        landed(sp.dma_start(out_t[T], a), "out", T)

    for T in range(NT):
        fetch(T)
    shared_readers.extend([shared_readers[-1]] * 2)
    tail = shared_work(range(MIDDLE, NT // GT), late_buf, [bank[4], bank[5], bank[0]])
    for i in range(NBLK - 3, NBLK):
        need(pe, "gT_out", i)
        need(act, f"y{i % NY}", i)
    for _ in range(3 * AHEAD):
        next(tail, None)
    for T in range(NT):
        for k in sum_up(T):
            if k % 2:
                for _ in range(3):
                    next(tail, None)
    need(sp, "out", NT - 1)
    ctx.close()


_INS = ["x", "Wq", "Wk", "Wv", "Wo", "bo", "router_w", "router_bias", "wg", "wu", "wd", "swg", "swu", "swd"]


def kernel(**inputs):
    import concourse.bacc as bacc
    from concourse.bass_utils import run_bass_kernel_spmd

    nc = bacc.Bacc("TRN2", target_bir_lowering=False, num_devices=1)
    (w32, c32), (w16, c16) = layout_constants()
    arrays = {f"in_{n}": np.ascontiguousarray(inputs[("L0_attn_" if n in ("x", "Wq", "Wk", "Wv", "Wo", "bo") else "L0_ffn_") + n])
              for n in _INS}
    arrays["const32"], arrays["const16"] = c32, c16
    args = [nc.dram_tensor(n, a.shape, mybir.dt.from_np(a.dtype), kind="ExternalInput").ap() for n, a in arrays.items()]
    out = nc.dram_tensor("out_0", (B, L, D), mybir.dt.float32, kind="ExternalOutput").ap()
    build(nc, *args, w32, w16, out)
    r = run_bass_kernel_spmd(nc, [arrays], core_ids=[0])
    return r.results[0]["out_0"]
```
